# Optimizing a Trainium2 kernel written in Bass

```python
import numpy as np
import jax
import jax.numpy as jnp

def _softmax(x, axis=-1):
    return jax.nn.softmax(x, axis=axis)
def _gelu(x):
    return jax.nn.gelu(x, approximate=True)
def _silu(x):
    return jax.nn.silu(x)
def _sigmoid(x):
    return jax.nn.sigmoid(x)
def _layernorm(x, axis=-1, eps=1e-5):
    m = jnp.mean(x, axis=axis, keepdims=True)
    v = jnp.var(x, axis=axis, keepdims=True)
    return (x - m) / jnp.sqrt(v + eps)
def _scatter_add(tgt, idx, src, axis=0):
    return tgt.at[idx].add(src)
def _segment_sum(src, seg, n):
    return jax.ops.segment_sum(src, seg, n)

kernel_name = 'mk_conv_seq_d2_conv_nchw128_168794'

def setup_inputs(seed: int = 0):
    np.random.seed(seed)
    _w = jnp.asarray
    def _rec_inputs():
        import jax
        import jax.numpy as jnp
        _gk = jax.random.key(seed)
        x = -0.0005207 + 1.001 * jax.random.normal(jax.random.fold_in(_gk, 1), (4, 128, 64, 64), jnp.float32)
        return x
    x = _rec_inputs()
    def _L0_conv_setup():
        import jax, jax.numpy as jnp
        import numpy as np
        key = jax.random.key(seed)
        ks = jax.random.split(key, 9)
        B, C, IC, H, W = (4, 128, 64, 64, 64)
        s = 0.05
        return {'x': jax.random.normal(ks[0], (B, C, H, W), dtype=jnp.float32), 'g_w': jax.random.normal(ks[1], (IC, C), dtype=jnp.float32) * s, 'g_b': jax.random.normal(ks[2], (IC,), dtype=jnp.float32) * s, 'theta_w': jax.random.normal(ks[3], (IC, C), dtype=jnp.float32) * s, 'theta_b': jax.random.normal(ks[4], (IC,), dtype=jnp.float32) * s, 'phi_w': jax.random.normal(ks[5], (IC, C), dtype=jnp.float32) * s, 'phi_b': jax.random.normal(ks[6], (IC,), dtype=jnp.float32) * s, 'W_w': jax.random.normal(ks[7], (C, IC), dtype=jnp.float32) * s, 'W_b': jax.random.normal(ks[8], (C,), dtype=jnp.float32) * s}
    _L0_conv_all = _L0_conv_setup()
    _L0_conv_in = {k: v for k, v in _L0_conv_all.items() if k in ('g_w', 'g_b', 'theta_w', 'theta_b', 'phi_w', 'phi_b', 'W_w', 'W_b', )}
    del _L0_conv_all

    def _L1_conv_setup():
        import jax, jax.numpy as jnp
        import numpy as np
        B, C, H, W = (8, 128, 64, 64)
        key = jax.random.key(seed)
        ks = jax.random.split(key, 7)
        s = 1.0 / np.sqrt(C)
        return {'x': jax.random.normal(ks[0], (B, C, H, W), dtype=jnp.float32), 'Wq': jax.random.normal(ks[1], (C, C), dtype=jnp.float32) * s, 'bq': jax.random.normal(ks[2], (C,), dtype=jnp.float32) * 0.01, 'Wk': jax.random.normal(ks[3], (C, C), dtype=jnp.float32) * s, 'bk': jax.random.normal(ks[4], (C,), dtype=jnp.float32) * 0.01, 'Wv': jax.random.normal(ks[5], (C, C), dtype=jnp.float32) * s, 'bv': jax.random.normal(ks[6], (C,), dtype=jnp.float32) * 0.01}
    _L1_conv_all = _L1_conv_setup()
    _L1_conv_in = {k: v for k, v in _L1_conv_all.items() if k in ('Wq', 'bq', 'Wk', 'bk', 'Wv', 'bv', )}
    del _L1_conv_all

    return {
        "x": x,
        "L0_conv_g_w": _L0_conv_in["g_w"],
        "L0_conv_g_b": _L0_conv_in["g_b"],
        "L0_conv_theta_w": _L0_conv_in["theta_w"],
        "L0_conv_theta_b": _L0_conv_in["theta_b"],
        "L0_conv_phi_w": _L0_conv_in["phi_w"],
        "L0_conv_phi_b": _L0_conv_in["phi_b"],
        "L0_conv_W_w": _L0_conv_in["W_w"],
        "L0_conv_W_b": _L0_conv_in["W_b"],
        "L1_conv_Wq": _L1_conv_in["Wq"],
        "L1_conv_bq": _L1_conv_in["bq"],
        "L1_conv_Wk": _L1_conv_in["Wk"],
        "L1_conv_bk": _L1_conv_in["bk"],
        "L1_conv_Wv": _L1_conv_in["Wv"],
        "L1_conv_bv": _L1_conv_in["bv"],
    }

def reference(x, L0_conv_g_w, L0_conv_g_b, L0_conv_theta_w, L0_conv_theta_b, L0_conv_phi_w, L0_conv_phi_b, L0_conv_W_w, L0_conv_W_b, L1_conv_Wq, L1_conv_bq, L1_conv_Wk, L1_conv_bk, L1_conv_Wv, L1_conv_bv):
    import jax
    import jax.numpy as jnp
    def _L0_conv_ref(x, g_w, g_b, theta_w, theta_b, phi_w, phi_b, W_w, W_b):
        import jax, jax.numpy as jnp
        import numpy as np
        B, C, H, Wd = x.shape
        N = H * Wd
        xf = x.reshape(B, C, N)
        g_x = jnp.einsum('ic,bcn->bni', g_w, xf) + g_b
        theta_x = jnp.einsum('ic,bcn->bni', theta_w, xf) + theta_b
        phi_x = jnp.einsum('ic,bcn->bin', phi_w, xf) + phi_b[None, :, None]
        f = jnp.einsum('bni,bim->bnm', theta_x, phi_x)
        f_div_C = jax.nn.softmax(f, axis=-1)
        y = jnp.einsum('bnm,bmi->bni', f_div_C, g_x)
        y = y.transpose(0, 2, 1)
        W_y = jnp.einsum('ci,bin->bcn', W_w, y) + W_b[None, :, None]
        return (W_y + xf).reshape(B, C, H, Wd)

    def _L1_conv_ref(x, Wq, bq, Wk, bk, Wv, bv):
        import jax, jax.numpy as jnp
        import numpy as np
        B, C, H, W = (8, 128, 64, 64)
        b, c, h, w = x.shape
        n = h * w
        scale = 1.0 / jnp.sqrt(jnp.asarray(c, x.dtype))
        xf = x.reshape(b, c, n)
        q = jnp.einsum('oc,bcn->bno', Wq, xf) + bq
        k = jnp.einsum('oc,bcn->bcn', Wk, xf) + bk[None, :, None]
        v = jnp.einsum('oc,bcn->bno', Wv, xf) + bv
        attn = jax.nn.softmax(jnp.einsum('bnc,bcm->bnm', q, k) * scale, axis=-1)
        out = jnp.einsum('bnm,bmc->bnc', attn, v)
        return x + out.transpose(0, 2, 1).reshape(b, c, h, w)

    def _gn(v, G=32, eps=1e-5):
        B_, C_, H_, W_ = v.shape
        g = v.reshape(B_, G, C_ // G, H_, W_)
        m = jnp.mean(g, axis=(2, 3, 4), keepdims=True)
        s = jnp.var(g, axis=(2, 3, 4), keepdims=True)
        return ((g - m) / jnp.sqrt(s + eps)).reshape(v.shape)

    def _ln_c(v, eps=1e-6):
        m = jnp.mean(v, axis=1, keepdims=True)
        s = jnp.var(v, axis=1, keepdims=True)
        return (v - m) / jnp.sqrt(s + eps)

    def _ln_t(v, eps=1e-5):
        m = jnp.mean(v, axis=-1, keepdims=True)
        s = jnp.var(v, axis=-1, keepdims=True)
        return (v - m) / jnp.sqrt(s + eps)

    def _to_tokens(v):
        B_, C_, H_, W_ = v.shape
        return v.reshape(B_, C_, H_ * W_).transpose(0, 2, 1)
    def _from_tokens(t, like):
        B_, C_, H_, W_ = like.shape
        return t.transpose(0, 2, 1).reshape(B_, C_, H_, W_)

    x = _L0_conv_ref(x, L0_conv_g_w, L0_conv_g_b, L0_conv_theta_w, L0_conv_theta_b, L0_conv_phi_w, L0_conv_phi_b, L0_conv_W_w, L0_conv_W_b)
    x = _L1_conv_ref(x, L1_conv_Wq, L1_conv_bq, L1_conv_Wk, L1_conv_bk, L1_conv_Wv, L1_conv_bv)
    return x


_drawn_inputs = setup_inputs


def setup_inputs(seed=0):
    import zlib

    import numpy as np

    out = dict(_drawn_inputs(seed))
    spreads = {}
    factors = {'L0_conv_theta_b': 5.541,
     'L0_conv_phi_b': 64.0,
     'L1_conv_bq': 64.0,
     'L1_conv_bk': 64.0,
     'L1_conv_bv': 5.367}
    for name, (base, spread) in spreads.items():
        noise = np.random.default_rng([zlib.crc32(name.encode()), seed]).standard_normal(out[name].shape)
        drawn = base * np.exp(spread * noise) if base else spread * noise
        out[name] = jnp.asarray(drawn.astype(out[name].dtype))
    for name, factor in factors.items():
        out[name] = (out[name] * factor).astype(out[name].dtype)
    return out
```

```python
from contextlib import ExitStack

import concourse.bass as bass
from concourse import mybir

ALU = mybir.AluOpType
ACT = mybir.ActivationFunctionType
AX = mybir.AxisListType
F32 = mybir.dt.float32
F32R = mybir.dt.float32r

P = 128
QB = 512
KT = 128
TPG = 2
GC = TPG * QB
SUB = QB // P
BUFS = 4
LAG = 2

PIECES_AT = [2 if s in (4, 9) else 1 if s < 14 else 0 for s in range(16)]
DIAG_AT = 14
ROW_AT = 15
POOL_ADDS = (1, 3, 5, 8, 10, 12)


def build(nc, x, wT_theta, b_theta, wT_phi, b_phi, wT_g, b_g, wT_out, b_out,
          wT_q, b_q, w_k, b_k, wT_v, b_v, ident, out):
    B, C, N = x.shape
    IC = wT_theta.shape[1]
    assert C == P and 2 * IC == P and N % (2 * QB) == 0
    BLOCKS = N // QB
    TILES = N // KT
    GROUPS = TILES // TPG
    PIECES = SUB * (N // GC)
    assert GROUPS == len(PIECES_AT) and sum(PIECES_AT) == PIECES
    CHUNKS = N // QB
    VSTEP = 2 * IC + 2
    G_PER_BANK = QB // IC
    V_PER_BANK = QB // C
    G_CHUNKS = TILES // G_PER_BANK
    V_CHUNKS = TILES // V_PER_BANK
    L0_CHUNKS = 2 * CHUNKS + G_CHUNKS
    L1_CHUNKS = CHUNKS + V_CHUNKS
    ALL_CHUNKS = L0_CHUNKS + L1_CHUNKS
    BANKS = 4
    assert L0_CHUNKS % BANKS == 0 and L1_CHUNKS % BANKS == 0
    SCALES = (1.0, float(C) ** -0.5)

    with ExitStack() as ctx:
        def sb(name, shape, dt=F32):
            return ctx.enter_context(nc.sbuf_tensor(name, shape, dt))

        def sem(name):
            return ctx.enter_context(nc.semaphore(name))

        scores = ctx.enter_context(nc.psum_tensor("scores", [P, 2, GC], F32))
        rough = ctx.enter_context(nc.psum_tensor("rough", [P, GC], F32))
        acc_out = ctx.enter_context(nc.psum_tensor("acc_out", [P, 2, QB], F32))
        proj = scores[:].rearrange("p a (b c) -> p (a b) c", c=QB)

        x_in = sb("x_in", [P, N])
        x_mid = sb("x_mid", [P, N])
        keys_a = sb("keys_a", [P, N], F32R)
        keys_b = sb("keys_b", [P, N], F32R)
        qry_a = sb("qry_a", [P, N], F32R)
        qry_b = sb("qry_b", [P, N], F32R)
        vals = sb("vals", [P, 2 * N], F32R)
        q_stage = sb("q_stage", [P, QB], F32R)
        probs = sb("probs", [P, 2, GC])
        probs_hi = sb("probs_hi", [P, BUFS, GC], F32R)
        probs_lo = sb("probs_lo", [P, BUFS, GC], F32R)
        whole = probs[:, :, 0:QB]
        diag = sb("diag", [P, 2, QB], F32R)
        piece_max = sb("piece_max", [P, SUB, N // GC])
        query_max = sb("query_max", [P, SUB])
        sums = sb("sums", [P, 2, GC])
        sums_pool = sb("sums_pool", [P, 2, GC])
        y_sb = sb("y_sb", [P, QB])
        o_sb = sb("o_sb", [P, QB])
        rden = sb("rden", [P, QB])
        result = sb("result", [P, 2, QB])
        wt_theta = sb("wt_theta", [P, P])
        wt_phi = sb("wt_phi", [P, P])
        wt_g = sb("wt_g", [P, IC])
        wt_out = sb("wt_out", [P, C])
        wt_q = sb("wt_q", [P, C])
        wk = sb("wk", [P, C])
        wt_v = sb("wt_v", [P, C])
        neg_ident = sb("neg_ident", [P, P])
        idt = sb("idt", [P, P])
        ones = sb("ones", [P, P])
        ones_r = sb("ones_r", [P, P], F32R)
        pick_den = sb("pick_den", [P, P])
        vec = sb("vec", [P, 8])
        TH_B, PHI_B, OUT_B, Q_B, K_B, V_B, K_S = (vec[:, i:i + 1] for i in range(7))
        g_bias = sb("g_bias", [P, 2])

        s_const = sem("s_const")
        s_set = sem("s_set")
        s_small = sem("s_small")
        s_vec = sem("s_vec")
        s_xin = sem("s_xin")
        s_proj = sem("s_proj")
        s_hi = sem("s_hi")
        s_lo = sem("s_lo")
        s_khi = sem("s_khi")
        s_plo = sem("s_plo")
        s_ones = sem("s_ones")
        s_settled = sem("s_settled")
        s_stage = sem("s_stage")
        s_rough = sem("s_rough")
        s_reduced = sem("s_reduced")
        s_qmax = sem("s_qmax")
        s_diag = sem("s_diag")
        s_row = sem("s_row")
        s_row_sb = sem("s_row_sb")
        s_scores = sem("s_scores")
        s_probs = sem("s_probs")
        s_split = sem("s_split")
        s_added = sem("s_added")
        s_plus = sem("s_plus")
        s_used = sem("s_used")
        s_y = sem("s_y")
        s_den = sem("s_den")
        s_rden = sem("s_rden")
        s_wy = sem("s_wy")
        s_norm = sem("s_norm")
        s_done = sem("s_done")
        s_stored = (sem("s_stored_even"), sem("s_stored_odd"))

        CONSTS = 19
        DVE_ADDS = [s for s in range(GROUPS) if s not in POOL_ADDS]
        assert 0 in DVE_ADDS and LAG == 2 and BUFS == 4
        LO_PARTS = 3 * CHUNKS
        POOL_PARTS = G_CHUNKS + CHUNKS + V_CHUNKS

        def lo_parts(n):
            return min(n, 2 * CHUNKS) + max(0, min(n - L0_CHUNKS, CHUNKS))

        def cols(t, i, n=QB):
            return t[:, bass.ds(i * n, n)] if not isinstance(i, int) else t[:, i * n:(i + 1) * n]

        def rd(ap):
            return ap.bitcast(F32)

        def g_hi(tile, n=1):
            return vals[:, tile * VSTEP:(tile + n) * VSTEP].rearrange("p (t c) -> p t c", c=VSTEP)[:, :, 0:IC]

        def g_lo(tile, n=1):
            return vals[:, tile * VSTEP:(tile + n) * VSTEP].rearrange("p (t c) -> p t c", c=VSTEP)[:, :, IC + 1:2 * IC + 1]

        def values_hi(layer, tile):
            return vals[:, tile * VSTEP:tile * VSTEP + P] if layer == 0 else vals[:, tile * P:(tile + 1) * P]

        def values_lo(layer, tile):
            if layer == 0:
                return vals[:, tile * VSTEP + IC + 1:tile * VSTEP + IC + 1 + P]
            return vals[:, N + tile * P:N + (tile + 1) * P]

        def each_block(eng, b, layer, block):
            base, own = b * (2 * BLOCKS) + layer * BLOCKS, b * BLOCKS
            block(base, own, 0, 0, True, False)
            with eng.Fori(0, BLOCKS // 2 - 1) as i:
                block(base + 2 * i + 1, own + 2 * i + 1, 2 * i + 1, 1, False, False)
                block(base + 2 * i + 2, own + 2 * i + 2, 2 * i + 2, 0, False, False)
            block(base + (BLOCKS - 1), own + (BLOCKS - 1), BLOCKS - 1, 1, False, True)

        block = ctx.enter_context(nc.Block())

        @block.sync
        def _(sp):
            sp.dma_start(x_in[:], x[0]).then_inc(s_xin, 16)
            sp.wait_ge(s_set, 4)
            for dst, src in (
                (wt_theta[:, 0:IC], wT_theta), (wt_theta[:, IC:P], wT_theta),
                (wt_phi[:, 0:IC], wT_phi), (wt_phi[:, IC:P], wT_phi),
                (vec[0:IC, 0:1], b_theta), (vec[IC:P, 0:1], b_theta),
                (vec[0:IC, 1:2], b_phi), (vec[IC:P, 1:2], b_phi),
                (wt_g[:], wT_g), (g_bias[0:IC, 0:1], b_g), (wt_out[0:IC, :], wT_out),
                (wt_q[:], wT_q), (wk[:], w_k), (wt_v[:], wT_v), (idt[:], ident),
                (vec[:, 3:4], b_q), (vec[:, 4:5], b_k), (vec[:, 5:6], b_v),
            ):
                sp.dma_start(dst, src).then_inc(s_const, 16)
            sp.dma_start(vec[:, 7:8], b_out).then_inc(s_const, 16)

            def store(b, blk, parity):
                sp.wait_ge(s_done, b * (2 * BLOCKS) + BLOCKS + blk + 3)
                dst = out[b] if isinstance(b, int) else out[bass.ds(b, 1)].rearrange("a c n -> (a c) n")
                sp.dma_start(cols(dst, blk), result[:, parity]).then_inc(s_stored[parity], 16)

            def image(b, more):
                if more:
                    sp.wait_ge(s_done, b * (2 * BLOCKS) + BLOCKS + 2)
                    nxt = x[bass.ds(b + 1, 1)].rearrange("a c n -> (a c) n")
                    sp.dma_start(x_in[:], nxt).then_inc(s_xin, 16)
                with sp.Fori(0, BLOCKS // 2) as i:
                    store(b, 2 * i, 0)
                    store(b, 2 * i + 1, 1)

            with sp.Fori(0, B - 1) as b:
                image(b, True)
            image(B - 1, False)
            for parity in range(2):
                sp.wait_ge(s_stored[parity], 16 + 16 * B * BLOCKS // 2)

        @block.tensor
        def _(pe):
            mm = nc.tensor.matmul

            pe.wait_ge(s_const, 16 * CONSTS)
            pe.wait_ge(s_set, 8)
            mm(rough[:, 0:2], wk[:], ones[:, 0:2], start=True, stop=True)
            mm(rough[:, QB:QB + 2], wt_out[:], g_bias[:], start=True, stop=True).then_inc(s_small, 1)
            pe.wait_ge(s_vec, 1)

            def project(n, b, lhsT, rhs):
                place = proj[:, n % BANKS]
                if n >= BANKS:
                    pe.wait_ge(s_hi, b * ALL_CHUNKS + n - BANKS + 1)
                    lo_before = lo_parts(n - BANKS + 1)
                    pe.wait_ge(s_lo, b * LO_PARTS + lo_before)
                for k, (l, r) in enumerate(zip(lhsT, rhs)):
                    w = QB // len(lhsT)
                    last = mm(place[:, k * w:(k + 1) * w], l, r, start=True, stop=True)
                last.then_inc(s_proj, 1)

            def rough_piece(g, m):
                kk, t = divmod(m, SUB)
                if m == 0:
                    pe.wait_ge(s_stage, g + 1)
                pe.wait_ge(s_reduced, g * PIECES + m + 1)
                for h in range(TPG):
                    c = kk * GC + h * QB
                    last = mm(rough[:, h * QB:(h + 1) * QB], q_stage[:, t * P:(t + 1) * P],
                              keys_a[:, c:c + QB], start=True, stop=True)
                last.then_inc(s_rough, 1)

            def shift_row(g, parity):
                pe.wait_ge(s_diag, g + 1)
                pe.wait_ge(s_done, g + 1)
                mm(acc_out[:, parity], ones_r[:], diag[:, parity], start=True, stop=True).then_inc(s_row, 1)

            def score_group(layer, g, blk, parity, s):
                pe.wait_ge(s_probs, (g * GROUPS + s) * 2 + 2)
                for h in range(TPG):
                    k = (s * TPG + h) * KT
                    place = scores[:, s % 2, h * QB:(h + 1) * QB]
                    mm(place, keys_a[:, k:k + KT], cols(qry_a, blk), start=True, stop=False)
                    if layer == 0:
                        last = mm(place, keys_b[0:IC + 1, k:k + KT], cols(qry_b[0:IC + 1], blk),
                                  start=False, stop=True)
                    else:
                        mm(place, keys_b[:, k:k + KT], cols(qry_a, blk), start=False, stop=False)
                        mm(place, keys_a[:, k:k + KT], cols(qry_b, blk), start=False, stop=False)
                        last = mm(place, ones_r[:], diag[:, parity], start=False, stop=True)
                last.then_inc(s_scores, 1)

            def value_group(layer, g, parity, s):
                if s == 0:
                    pe.wait_ge(s_done, g + 1)
                pe.wait_ge(s_split, g * GROUPS + s + 3)
                for h in range(TPG):
                    tile = s * TPG + h
                    hi = probs_hi[:, s % BUFS, h * QB:(h + 1) * QB]
                    lo = probs_lo[:, s % BUFS, h * QB:(h + 1) * QB]
                    o = acc_out[:, parity]
                    mm(o, values_hi(layer, tile), hi, start=tile == 0, stop=False)
                    mm(o, values_lo(layer, tile), hi, start=False, stop=False)
                    last = mm(o, values_hi(layer, tile), lo, start=False, stop=tile == TILES - 1)
                last.then_inc(s_used, 1)

            def denominators(layer, g, nth, parity):
                pe.wait_ge(s_y, g + 1)
                o = acc_out[:, parity]
                if layer == 0:
                    mm(o, pick_den[:], y_sb[:], start=True, stop=True).then_inc(s_den, 1)
                    return
                pe.wait_ge(s_added, (nth + 2) * len(DVE_ADDS))
                pe.wait_ge(s_plus, (nth + 2) * len(POOL_ADDS))
                parts = [t[:, parity, h * QB:(h + 1) * QB] for t in (sums, sums_pool) for h in range(TPG)]
                for k, part in enumerate(parts):
                    last = mm(o, ones[:], part, start=k == 0, stop=k == len(parts) - 1)
                last.then_inc(s_den, 1)

            def out_projection(g, parity):
                pe.wait_ge(s_rden, g + 1)
                mm(acc_out[:, parity], wt_out[:], y_sb[:], start=True, stop=True).then_inc(s_wy, 1)

            with pe.Fori(0, B) as b:
                for layer in range(2):
                    g0 = b * (2 * BLOCKS) + layer * BLOCKS
                    pe.wait_ge(s_probs, g0 * (2 * GROUPS) + 4)
                    if layer == 0:
                        pe.wait_ge(s_xin, b * 16 + 16)
                        n = 0
                        project(n, b, [wt_theta[:]], [x_in[:, 0:QB]])
                        for c in range(CHUNKS):
                            n += 1
                            project(n, b, [wt_phi[:]], [x_in[:, c * QB:(c + 1) * QB]])
                            if c % TPG == TPG - 1:
                                pe.wait_ge(s_hi, b * ALL_CHUNKS + n + 1)
                                pe.wait_ge(s_lo, b * LO_PARTS + n + 1)
                                for t in range(SUB):
                                    rough_piece(g0, c // TPG * SUB + t)
                        for c in range(1, CHUNKS):
                            n += 1
                            project(n, b, [wt_theta[:]], [x_in[:, c * QB:(c + 1) * QB]])
                        for c in range(G_CHUNKS):
                            n += 1
                            project(n, b, [x_in[:, (c * G_PER_BANK + k) * KT:(c * G_PER_BANK + k + 1) * KT]
                                           for k in range(G_PER_BANK)], [wt_g[:]] * G_PER_BANK)
                        shift_row(g0, 0)
                        pe.wait_ge(s_hi, b * ALL_CHUNKS + L0_CHUNKS)
                        pe.wait_ge(s_lo, b * LO_PARTS + lo_parts(L0_CHUNKS))
                        pe.wait_ge(s_plo, b * POOL_PARTS + G_CHUNKS)
                        pe.wait_ge(s_ones, b * 4 + 4)
                    else:
                        pe.wait_ge(s_done, g0 + 2)
                        for c in range(CHUNKS):
                            project(L0_CHUNKS + c, b, [wt_q[:]], [x_mid[:, c * QB:(c + 1) * QB]])
                            if c % TPG == TPG - 1:
                                pe.wait_ge(s_khi, b * CHUNKS + c + 1)
                                for t in range(SUB):
                                    rough_piece(g0, c // TPG * SUB + t)
                        for c in range(V_CHUNKS):
                            project(L0_CHUNKS + CHUNKS + c, b,
                                    [x_mid[:, (c * V_PER_BANK + k) * KT:(c * V_PER_BANK + k + 1) * KT]
                                     for k in range(V_PER_BANK)], [wt_v[:]] * V_PER_BANK)
                        pe.wait_ge(s_diag, g0 + 1)
                        pe.wait_ge(s_hi, b * ALL_CHUNKS + ALL_CHUNKS)
                        pe.wait_ge(s_lo, b * LO_PARTS + LO_PARTS)
                        pe.wait_ge(s_plo, (b + 1) * POOL_PARTS)

                    def blk_program(g, nth, blk, parity, first, last, layer=layer):
                        m = 0
                        for s in range(GROUPS):
                            if s == ROW_AT and layer == 0 and not last:
                                shift_row(g + 1, 1 - parity)
                            if s == 0 and layer == 0:
                                pe.wait_ge(s_row_sb, nth + 1)
                            if s == 0 and layer == 1:
                                pe.wait_ge(s_diag, g + 1)
                            score_group(layer, g, blk, parity, s)
                            if not last:
                                for _ in range(PIECES_AT[s]):
                                    rough_piece(g + 1, m)
                                    m += 1
                            if not first and s == 3:
                                denominators(layer, g - 1, nth - 1, 1 - parity)
                            if not first and s == 5 and layer == 0:
                                out_projection(g - 1, 1 - parity)
                            if s >= LAG:
                                value_group(layer, g, parity, s - LAG)
                            elif not first:
                                value_group(layer, g - 1, 1 - parity, GROUPS + s - LAG)
                        if last:
                            for s in range(GROUPS - LAG, GROUPS):
                                value_group(layer, g, parity, s)
                            denominators(layer, g, nth, parity)
                            if layer == 0:
                                out_projection(g, parity)

                    each_block(pe, b, layer, blk_program)

        @block.scalar
        def _(act):
            def copy(dst, src, bias=None, scale=1.0):
                if bias is None:
                    return nc.scalar.activation(dst, src, ACT.Copy)
                return nc.scalar.activation(dst, src, ACT.Identity, bias=bias, scale=scale)

            def landed(b, n):
                act.wait_ge(s_proj, b * ALL_CHUNKS + n + 1)
                return proj[:, n % BANKS]

            def whole_free(b, w):
                if w >= 2:
                    act.wait_ge(s_plo, b * POOL_PARTS + w - 1)
                return whole[:, w % 2]

            def shift_to_row(nth, blk, parity):
                act.wait_ge(s_row, nth + 1)
                copy(cols(qry_b[IC:IC + 1], blk), acc_out[IC:IC + 1, parity]).then_inc(s_row_sb, 1)

            def take_output(layer, g, parity):
                act.wait_ge(s_used, (g + 1) * GROUPS + BUFS)
                act.wait_ge(s_done, g + 2)
                if layer == 0:
                    copy(y_sb[0:IC + 1], acc_out[0:IC + 1, parity]).then_inc(s_y, 1)
                else:
                    copy(o_sb[:], acc_out[:, parity]).then_inc(s_y, 1)

            def exponentials(layer, g, nth, s):
                n = g * GROUPS + s
                act.wait_ge(s_scores, n + 1)
                act.wait_ge(s_split, n + 1)
                if layer == 1:
                    before, blocks = (s - 2) % GROUPS, nth + (1 if s >= 2 else 0)
                    if before in POOL_ADDS:
                        act.wait_ge(s_plus, blocks * len(POOL_ADDS) + POOL_ADDS.index(before) + 1)
                    else:
                        act.wait_ge(s_added, blocks * len(DVE_ADDS) + DVE_ADDS.index(before) + 1)
                nc.scalar.activation(probs[:, s % 2], scores[:, s % 2], ACT.Exp,
                                     scale=SCALES[layer]).then_inc(s_probs, 1)
                act.wait_ge(s_used, n + 1)
                nc.scalar.activation(probs_hi[:, s % BUFS], scores[:, s % 2], ACT.Exp,
                                     scale=SCALES[layer]).then_inc(s_probs, 1)

            act.wait_ge(s_const, 16 * CONSTS)
            act.wait_ge(s_vec, 2)
            with act.Fori(0, B) as b:
                for layer in range(2):
                    g0 = b * (2 * BLOCKS) + layer * BLOCKS
                    act.wait_ge(s_used, g0 * GROUPS + BUFS)
                    if layer == 0:
                        n = 0
                        copy(qry_a[:, 0:QB], landed(b, n), TH_B).then_inc(s_hi, 1)
                        for c in range(CHUNKS):
                            n += 1
                            src = landed(b, n)
                            copy(keys_a[0:IC, c * QB:(c + 1) * QB], src[0:IC], PHI_B[0:IC])
                            copy(keys_b[:, c * QB:(c + 1) * QB], src, PHI_B).then_inc(s_hi, 1)
                        for c in range(1, CHUNKS):
                            n += 1
                            copy(qry_a[:, c * QB:(c + 1) * QB], landed(b, n), TH_B).then_inc(s_hi, 1)
                        for c in range(G_CHUNKS):
                            n += 1
                            src = landed(b, n)
                            copy(whole_free(b, c), src)
                            copy(g_hi(c * G_PER_BANK, G_PER_BANK),
                                 src.rearrange("p (t c) -> p t c", c=IC)).then_inc(s_hi, 1)
                        shift_to_row(b * BLOCKS, 0, 0)
                    else:
                        act.wait_ge(s_done, g0 + 2)
                        for c in range(CHUNKS):
                            w = G_CHUNKS + c
                            src = x_mid[:, c * QB:(c + 1) * QB]
                            copy(whole_free(b, w), src, K_B, K_S)
                            copy(keys_a[:, c * QB:(c + 1) * QB], src, K_B, K_S).then_inc(s_khi, 1)
                            copy(qry_a[:, c * QB:(c + 1) * QB], landed(b, L0_CHUNKS + c), Q_B).then_inc(s_hi, 1)
                        for c in range(V_CHUNKS):
                            src = landed(b, L0_CHUNKS + CHUNKS + c)
                            copy(whole_free(b, G_CHUNKS + CHUNKS + c), src)
                            copy(vals[:, c * QB:(c + 1) * QB], src).then_inc(s_hi, 1)
                    act.wait_ge(s_plo, b * POOL_PARTS + (G_CHUNKS if layer == 0 else POOL_PARTS))

                    def blk_program(g, nth, blk, parity, first, last, layer=layer):
                        for s in range(GROUPS):
                            if s == ROW_AT and layer == 0 and not last:
                                shift_to_row(nth + 1, blk + 1, 1 - parity)
                            if s == 2 and not first:
                                take_output(layer, g - 1, 1 - parity)
                            exponentials(layer, g, nth, s)
                        if last:
                            take_output(layer, g, parity)

                    each_block(act, b, layer, blk_program)

        @block.vector
        def _(dve):
            def piece(g, m):
                kk, t = divmod(m, SUB)
                dve.wait_ge(s_rough, g * PIECES + m + 1)
                nc.vector.reduce_max(piece_max[:, t, kk:kk + 1], rough[:], AX.X).then_inc(s_reduced, 1)

            def shift(g, parity):
                dve.wait_ge(s_reduced, (g + 1) * PIECES + 1)
                nc.vector.reduce_max(query_max[:], piece_max[:], AX.X).then_inc(s_qmax, 1)
                dve.wait_ge(s_qmax, g + 1)
                nc.vector.tensor_tensor(
                    diag[:, parity].rearrange("p (t c) -> p t c", c=P),
                    neg_ident[:].unsqueeze(1).to_broadcast([P, SUB, P]),
                    query_max[:].unsqueeze(2).to_broadcast([P, SUB, P]), ALU.mult).then_inc(s_diag, 1)

            def split(g, s):
                n = g * GROUPS + s
                dve.wait_ge(s_probs, 2 * n + 6)
                dve.wait_ge(s_used, n + 1)
                nc.vector.tensor_tensor(probs_lo[:, s % BUFS], probs[:, s % 2], rd(probs_hi[:, s % BUFS]),
                                        ALU.subtract).then_inc(s_split, 1)

            def add(nth, parity, s):
                if s not in DVE_ADDS:
                    return
                k = DVE_ADDS.index(s)
                if k == 0:
                    nc.vector.tensor_copy(sums[:, parity], probs[:, s % 2]).then_inc(s_added, 1)
                    return
                dve.wait_ge(s_added, (nth + 1) * len(DVE_ADDS) + k)
                nc.vector.tensor_tensor(sums[:, parity], sums[:, parity], probs[:, s % 2],
                                        ALU.add).then_inc(s_added, 1)

            def reciprocals(g, parity):
                dve.wait_ge(s_den, g + 1)
                nc.vector.reciprocal(rden[:], acc_out[:, parity]).then_inc(s_rden, 1)

            def finish(layer, g, nth, blk, parity):
                if layer == 0:
                    dve.wait_ge(s_wy, nth + 1)
                    nc.vector.tensor_tensor(rden[:], acc_out[:, parity], rden[:], ALU.mult).then_inc(s_norm, 1)
                    dve.wait_ge(s_norm, g + 1)
                    nc.vector.scalar_tensor_tensor(out=cols(x_mid, blk), in0=rden[:], scalar=OUT_B,
                                                   in1=cols(x_in, blk), op0=ALU.add, op1=ALU.add).then_inc(s_done, 1)
                else:
                    dve.wait_ge(s_stored[parity], 8 * (nth - parity) + 16)
                    dve.wait_ge(s_rden, g + 1)
                    nc.vector.tensor_tensor(result[:, parity], o_sb[:], rden[:], ALU.mult).then_inc(s_norm, 1)
                    dve.wait_ge(s_norm, g + 1)
                    nc.vector.scalar_tensor_tensor(out=result[:, parity], in0=result[:, parity], scalar=V_B,
                                                   in1=cols(x_mid, blk), op0=ALU.add, op1=ALU.add).then_inc(s_done, 1)

            for free, n in ((s_reduced, 1), (s_probs, 4), (s_split, 2), (s_added, len(DVE_ADDS)),
                            (s_plus, len(POOL_ADDS)), (s_used, BUFS), (s_done, 2),
                            (s_stored[0], 16), (s_stored[1], 16)):
                dve.sem_inc(free, n)
            nc.vector.memset(ones[:], 1.0).then_inc(s_set, 1)
            nc.vector.memset(y_sb[:], 0.0).then_inc(s_set, 1)
            nc.vector.memset(g_bias[:], 0.0).then_inc(s_set, 1)
            nc.vector.memset(wt_out[:], 0.0).then_inc(s_set, 1)
            nc.vector.memset(pick_den[:], 0.0).then_inc(s_set, 1)
            dve.wait_ge(s_set, 5)
            nc.vector.memset(pick_den[IC:IC + 1, :], 1.0).then_inc(s_set, 1)
            nc.vector.tensor_copy(ones_r[:], ones[:]).then_inc(s_set, 1)
            dve.wait_ge(s_const, 16 * CONSTS)
            nc.vector.tensor_scalar(neg_ident[:], idt[:], -1.0, None, ALU.mult).then_inc(s_set, 1)
            dve.wait_ge(s_set, 8)
            dve.wait_ge(s_small, 1)
            nc.vector.tensor_copy(K_S, rough[:, 0:1]).then_inc(s_vec, 1)
            nc.vector.tensor_tensor(OUT_B, rough[:, QB:QB + 1], vec[:, 7:8], ALU.add).then_inc(s_vec, 1)
            dve.wait_ge(s_vec, 2)

            def taken(b, n):
                dve.wait_ge(s_hi, b * ALL_CHUNKS + n + 1)
                return proj[:, n % BANKS]

            def lo_part(dst, src, bias, hi):
                nc.vector.scalar_tensor_tensor(out=dst, in0=src, scalar=bias, in1=rd(hi),
                                               op0=ALU.add, op1=ALU.subtract).then_inc(s_lo, 1)

            with dve.Fori(0, B) as b:
                for layer in range(2):
                    g0 = b * (2 * BLOCKS) + layer * BLOCKS
                    if layer == 0:
                        n = 0
                        lo_part(qry_b[0:IC, 0:QB], taken(b, n)[0:IC], TH_B[0:IC], qry_a[0:IC, 0:QB])
                        for c in range(CHUNKS):
                            n += 1
                            at = slice(c * QB, (c + 1) * QB)
                            lo_part(keys_a[IC:P, at], taken(b, n)[IC:P], PHI_B[IC:P], keys_b[IC:P, at])
                            if c % TPG == TPG - 1:
                                for t in range(SUB):
                                    piece(g0, c // TPG * SUB + t)
                        shift(g0, 0)
                        for c in range(1, CHUNKS):
                            n += 1
                            at = slice(c * QB, (c + 1) * QB)
                            lo_part(qry_b[0:IC, at], taken(b, n)[0:IC], TH_B[0:IC], qry_a[0:IC, at])
                    else:
                        for c in range(CHUNKS):
                            at = slice(c * QB, (c + 1) * QB)
                            lo_part(qry_b[:, at], taken(b, L0_CHUNKS + c), Q_B, qry_a[:, at])
                            if c % TPG == TPG - 1:
                                for t in range(SUB):
                                    piece(g0, c // TPG * SUB + t)
                        shift(g0, 0)

                    def blk_program(g, nth, blk, parity, first, last, layer=layer):
                        m = 0
                        for s in range(GROUPS):
                            if s == DIAG_AT and not last:
                                shift(g + 1, 1 - parity)
                            if not last:
                                for _ in range(PIECES_AT[s]):
                                    piece(g + 1, m)
                                    m += 1
                            if s > 0:
                                split(g, s - 1)
                                if layer == 1:
                                    add(nth, parity, s - 1)
                            elif not first:
                                split(g - 1, GROUPS - 1)
                                if layer == 1:
                                    add(nth - 1, 1 - parity, GROUPS - 1)
                            if s == 4 and not first:
                                reciprocals(g - 1, 1 - parity)
                            if s == 6 and not first:
                                finish(layer, g - 1, nth - 1, blk - 1, 1 - parity)
                        if last:
                            split(g, GROUPS - 1)
                            if layer == 1:
                                add(nth, parity, GROUPS - 1)
                            reciprocals(g, parity)
                            finish(layer, g, nth, blk, parity)

                    each_block(dve, b, layer, blk_program)

        @block.gpsimd
        def _(pool):
            def settle():
                pool.sem_inc(s_settled, 1)

            def stage(g, blk):
                pool.wait_ge(s_reduced, g * PIECES + 1)
                settle()
                nc.gpsimd.tensor_copy(q_stage[:], rd(cols(qry_a, blk))).then_inc(s_stage, 1)

            def lo_part(dst, w, hi):
                nc.gpsimd.tensor_tensor(dst, w, rd(hi), ALU.subtract).then_inc(s_plo, 1)

            def add(g, nth, parity, s):
                k = POOL_ADDS.index(s)
                pool.wait_ge(s_probs, (g * GROUPS + s) * 2 + 5)
                if k == 0:
                    pool.wait_ge(s_done, g + 1)
                    settle()
                    nc.gpsimd.tensor_copy(sums_pool[:, parity], probs[:, s % 2]).then_inc(s_plus, 1)
                    return
                pool.wait_ge(s_plus, (nth + 1) * len(POOL_ADDS) + k)
                nc.gpsimd.tensor_tensor(sums_pool[:, parity], sums_pool[:, parity], probs[:, s % 2],
                                        ALU.add).then_inc(s_plus, 1)

            with pool.Fori(0, B) as b:
                for layer in range(2):
                    g0 = b * (2 * BLOCKS) + layer * BLOCKS
                    pool.wait_ge(s_used, g0 * GROUPS + BUFS)
                    first_q = 0 if layer == 0 else L0_CHUNKS
                    pool.wait_ge(s_hi, b * ALL_CHUNKS + first_q + 1)
                    stage(g0, 0)
                    if layer == 0:
                        tiles = vals[:, 0:TILES * VSTEP].bitcast(F32).rearrange("p (t c) -> p t c", c=VSTEP)
                        nc.gpsimd.memset(tiles[:, :, IC:IC + 1], 1.0).then_inc(s_ones, 1)
                        nc.gpsimd.memset(tiles[:, :, 2 * IC + 1:VSTEP], 0.0).then_inc(s_ones, 1)
                        nc.gpsimd.memset(vals[:, TILES * VSTEP:TILES * VSTEP + P].bitcast(F32), 0.0).then_inc(s_ones, 1)
                        pool.wait_ge(s_ones, b * 4 + 3)
                        pool.wait_ge(s_lo, b * LO_PARTS + CHUNKS + 1)
                        settle()
                        nc.gpsimd.memset(keys_b[IC:IC + 1, :].bitcast(F32), 1.0).then_inc(s_ones, 1)
                        pool.wait_ge(s_ones, b * 4 + 4)
                        for c in range(G_CHUNKS):
                            pool.wait_ge(s_hi, b * ALL_CHUNKS + 2 * CHUNKS + c + 1)
                            lo_part(g_lo(c * G_PER_BANK, G_PER_BANK),
                                    whole[:, c % 2].rearrange("p (t c) -> p t c", c=IC),
                                    g_hi(c * G_PER_BANK, G_PER_BANK))
                    else:
                        for c in range(CHUNKS):
                            at = slice(c * QB, (c + 1) * QB)
                            pool.wait_ge(s_khi, b * CHUNKS + c + 1)
                            lo_part(keys_b[:, at], whole[:, (G_CHUNKS + c) % 2], keys_a[:, at])
                        for c in range(V_CHUNKS):
                            at = slice(c * QB, (c + 1) * QB)
                            pool.wait_ge(s_hi, b * ALL_CHUNKS + L0_CHUNKS + CHUNKS + c + 1)
                            lo_part(vals[:, N + c * QB:N + (c + 1) * QB],
                                    whole[:, (G_CHUNKS + CHUNKS + c) % 2], vals[:, at])

                    def blk_program(g, nth, blk, parity, first, last, layer=layer):
                        if not last:
                            stage(g + 1, blk + 1)
                        if layer == 1:
                            for s in POOL_ADDS:
                                add(g, nth, parity, s)

                    each_block(pool, b, layer, blk_program)


def kernel(x, L0_conv_g_w, L0_conv_g_b, L0_conv_theta_w, L0_conv_theta_b, L0_conv_phi_w, L0_conv_phi_b,
           L0_conv_W_w, L0_conv_W_b, L1_conv_Wq, L1_conv_bq, L1_conv_Wk, L1_conv_bk, L1_conv_Wv, L1_conv_bv):
    import numpy as np
    import concourse.bacc as bacc
    from concourse.bass_utils import run_bass_kernel_spmd

    def turned(w):
        return np.ascontiguousarray(np.asarray(w).T)

    def column(v):
        return np.asarray(v).reshape(-1, 1)

    shape = np.shape(x)
    arrays = {
        "x": np.ascontiguousarray(np.asarray(x).reshape(shape[0], shape[1], -1)),
        "wT_theta": turned(L0_conv_theta_w), "b_theta": column(L0_conv_theta_b),
        "wT_phi": turned(L0_conv_phi_w), "b_phi": column(L0_conv_phi_b),
        "wT_g": turned(L0_conv_g_w), "b_g": column(L0_conv_g_b),
        "wT_out": turned(L0_conv_W_w), "b_out": column(L0_conv_W_b),
        "wT_q": turned(L1_conv_Wq), "b_q": column(L1_conv_bq),
        "w_k": np.asarray(L1_conv_Wk), "b_k": column(L1_conv_bk),
        "wT_v": turned(L1_conv_Wv), "b_v": column(L1_conv_bv),
        "ident": np.eye(P, dtype=np.float32),
    }
    nc = bacc.Bacc("TRN2", target_bir_lowering=False, num_devices=1)
    args = {n: nc.dram_tensor(n, a.shape, mybir.dt.from_np(a.dtype), kind="ExternalInput").ap()
            for n, a in arrays.items()}
    out = nc.dram_tensor("out", arrays["x"].shape, F32, kind="ExternalOutput").ap()
    build(nc, out=out, **args)
    r = run_bass_kernel_spmd(nc, [arrays], core_ids=[0])
    return r.results[0]["out"].reshape(shape)
```

```python
from contextlib import ExitStack

import concourse.bass as bass
from concourse import mybir

ALU = mybir.AluOpType
ACT = mybir.ActivationFunctionType
AX = mybir.AxisListType
F32 = mybir.dt.float32
F32R = mybir.dt.float32r

P = 128
QB = 512
KT = 128
TPG = 2
GC = TPG * QB
SUB = QB // P
BUFS = 4
LAG = 2

PIECES_AT = [2 if s in (9, 11) else 1 if s < 14 else 0 for s in range(16)]
DIAG_AT = 14
ROW_AT = 15
POOL_ADDS = (2, 4, 6, 8, 10, 12)


def build(nc, x, wT_theta, b_theta, wT_phi, b_phi, wT_g, b_g, wT_out, b_out,
          wT_q, b_q, w_k, b_k, wT_v, b_v, ident, out):
    B, C, N = x.shape
    IC = wT_theta.shape[1]
    assert C == P and 2 * IC == P and N % (2 * QB) == 0
    BLOCKS = N // QB
    TILES = N // KT
    GROUPS = TILES // TPG
    PIECES = SUB * (N // GC)
    assert GROUPS == len(PIECES_AT) and sum(PIECES_AT) == PIECES
    CHUNKS = N // QB
    VSTEP = 2 * IC + 2
    G_PER_BANK = QB // IC
    V_PER_BANK = QB // C
    G_CHUNKS = TILES // G_PER_BANK
    V_CHUNKS = TILES // V_PER_BANK
    L0_CHUNKS = 2 * CHUNKS + G_CHUNKS
    L1_CHUNKS = CHUNKS + V_CHUNKS
    ALL_CHUNKS = L0_CHUNKS + L1_CHUNKS
    assert V_CHUNKS == CHUNKS and G_CHUNKS == CHUNKS // TPG
    BANKS = 4
    assert L0_CHUNKS % BANKS == 0 and L1_CHUNKS % BANKS == 0
    SCALES = (1.0, float(C) ** -0.5)

    with ExitStack() as ctx:
        def sb(name, shape, dt=F32):
            return ctx.enter_context(nc.sbuf_tensor(name, shape, dt))

        def sem(name):
            return ctx.enter_context(nc.semaphore(name))

        scores = ctx.enter_context(nc.psum_tensor("scores", [P, 2, GC], F32))
        rough = ctx.enter_context(nc.psum_tensor("rough", [P, GC], F32))
        acc_out = ctx.enter_context(nc.psum_tensor("acc_out", [P, 2, QB], F32))
        proj = scores[:].rearrange("p a (b c) -> p (a b) c", c=QB)

        x_in = sb("x_in", [P, N])
        x_mid = sb("x_mid", [P, N])
        keys_a = sb("keys_a", [P, N], F32R)
        keys_b = sb("keys_b", [P, N], F32R)
        qry_a = sb("qry_a", [P, N], F32R)
        qry_b = sb("qry_b", [P, N], F32R)
        vals = sb("vals", [P, 2 * N], F32R)
        q_stage = sb("q_stage", [P, QB], F32R)
        probs = sb("probs", [P, 2, GC])
        probs_hi = sb("probs_hi", [P, BUFS, GC], F32R)
        probs_lo = sb("probs_lo", [P, BUFS, GC], F32R)
        whole = probs[:, :, 0:QB]
        diag = sb("diag", [P, 2, QB], F32R)
        piece_max = sb("piece_max", [P, SUB, N // GC])
        query_max = sb("query_max", [P, SUB])
        sums = sb("sums", [P, 2, GC])
        sums_pool = sb("sums_pool", [P, 2, GC])
        y_sb = sb("y_sb", [P, QB])
        o_sb = sb("o_sb", [P, QB])
        rcol = sb("rcol", [P, SUB])
        rdiag = sb("rdiag", [P, QB])
        result = sb("result", [P, 2, QB])
        wt_theta = sb("wt_theta", [P, P])
        wt_phi = sb("wt_phi", [P, P])
        wt_g = sb("wt_g", [P, IC])
        wt_out = sb("wt_out", [P, C])
        wt_q = sb("wt_q", [P, C])
        wk = sb("wk", [P, C])
        wt_v = sb("wt_v", [P, C])
        neg_ident = sb("neg_ident", [P, P])
        idt = sb("idt", [P, P])
        ones = sb("ones", [P, P])
        ones_r = sb("ones_r", [P, P], F32R)
        pick_den = sb("pick_den", [P, P])
        vec = sb("vec", [P, 8])
        TH_B, PHI_B, OUT_B, Q_B, K_B, V_B, K_S = (vec[:, i:i + 1] for i in range(7))
        g_bias = sb("g_bias", [P, 2])

        s_const = sem("s_const")
        s_set = sem("s_set")
        s_small = sem("s_small")
        s_vec = sem("s_vec")
        s_xin = sem("s_xin")
        s_proj = sem("s_proj")
        s_hi = sem("s_hi")
        s_lo = sem("s_lo")
        s_plo = sem("s_plo")
        s_ones = sem("s_ones")
        s_settled = sem("s_settled")
        s_stage = sem("s_stage")
        s_rough = sem("s_rough")
        s_reduced = sem("s_reduced")
        s_qmax = sem("s_qmax")
        s_diag = sem("s_diag")
        s_row = sem("s_row")
        s_row_sb = sem("s_row_sb")
        s_scores = sem("s_scores")
        s_probs = sem("s_probs")
        s_split = sem("s_split")
        s_added = sem("s_added")
        s_plus = sem("s_plus")
        s_used = sem("s_used")
        s_y = sem("s_y")
        s_fold = sem("s_fold")
        s_den = sem("s_den")
        s_rcol = sem("s_rcol")
        s_rdiag = sem("s_rdiag")
        s_rden = sem("s_rden")
        s_wy = sem("s_wy")
        s_norm = sem("s_norm")
        s_done = sem("s_done")
        s_stored = (sem("s_stored_even"), sem("s_stored_odd"))

        CONSTS = 19
        DVE_ADDS = [s for s in range(GROUPS) if s not in POOL_ADDS]
        assert 0 in DVE_ADDS and LAG == 2 and BUFS == 4
        def piece_run(kk, between):
            events = []
            for t in range(SUB):
                events += [("piece", kk * SUB + t)] + between[t]
            return events

        BETWEEN = ([("theta", 0), ("phi", 0), ("phi", 1)], [("k", 0), ("q", 0), ("k", 1)])
        for kk in range(CHUNKS // TPG):
            c = TPG * kk
            more = c + 2 < CHUNKS
            BETWEEN[0].extend(piece_run(kk, [
                [("phi", c + 2)] * more + [("theta", c + 1)], [("phi", c + 3)] * more,
                [("theta", c + 2)] * more, [("g", kk)]]))
            BETWEEN[1].extend(piece_run(kk, [
                [("k", c + 2)] * more + [("q", c + 1)], [("k", c + 3), ("v", c)] if more else [("v", c)],
                [("q", c + 2)] * more, [("v", c + 1)]]))

        def by_pool(kind, c):
            return kind in ("g", "k", "v") or (kind, c) == ("theta", c) and c > 0

        CHUNK, HI, DVE_LO, POOL_LO, WHOLE = {}, {}, {}, {}, {}
        dve_before, chunk_list = [0], []
        for layer, events in enumerate(BETWEEN):
            n_whole = 0
            for kind, c in events:
                if kind == "piece":
                    continue
                HI[kind, c] = len(HI)
                if kind != "k":
                    CHUNK[kind, c] = len(CHUNK)
                    chunk_list.append((kind, c))
                if by_pool(kind, c):
                    POOL_LO[kind, c] = len(POOL_LO)
                    WHOLE[kind, c] = n_whole
                    n_whole += 1
                else:
                    DVE_LO[kind, c] = len(DVE_LO)
        assert len(CHUNK) == ALL_CHUNKS
        POOL_L0 = sum(k in ("theta", "g") for k, _ in POOL_LO)
        HI_L0 = sum(k in ("theta", "phi", "g") for k, _ in HI)
        DVE_L0 = sum(k in ("theta", "phi") for k, _ in DVE_LO)

        def ready(eng, b, kind, c, lo=True):
            eng.wait_ge(s_hi, b * len(HI) + HI[kind, c] + 1)
            if lo and (kind, c) in DVE_LO:
                eng.wait_ge(s_lo, b * len(DVE_LO) + DVE_LO[kind, c] + 1)

        def cols(t, i, n=QB):
            return t[:, bass.ds(i * n, n)] if not isinstance(i, int) else t[:, i * n:(i + 1) * n]

        def rd(ap):
            return ap.bitcast(F32)

        def g_hi(tile, n=1):
            return vals[:, tile * VSTEP:(tile + n) * VSTEP].rearrange("p (t c) -> p t c", c=VSTEP)[:, :, 0:IC]

        def g_lo(tile, n=1):
            return vals[:, tile * VSTEP:(tile + n) * VSTEP].rearrange("p (t c) -> p t c", c=VSTEP)[:, :, IC + 1:2 * IC + 1]

        def values_hi(layer, tile):
            return vals[:, tile * VSTEP:tile * VSTEP + P] if layer == 0 else vals[:, tile * P:(tile + 1) * P]

        def values_lo(layer, tile):
            if layer == 0:
                return vals[:, tile * VSTEP + IC + 1:tile * VSTEP + IC + 1 + P]
            return vals[:, N + tile * P:N + (tile + 1) * P]

        def each_block(eng, b, layer, block):
            base, own = b * (2 * BLOCKS) + layer * BLOCKS, b * BLOCKS
            block(base, own, 0, 0, True, False)
            with eng.Fori(0, BLOCKS // 2 - 1) as i:
                block(base + 2 * i + 1, own + 2 * i + 1, 2 * i + 1, 1, False, False)
                block(base + 2 * i + 2, own + 2 * i + 2, 2 * i + 2, 0, False, False)
            block(base + (BLOCKS - 1), own + (BLOCKS - 1), BLOCKS - 1, 1, False, True)

        block = ctx.enter_context(nc.Block())

        @block.sync
        def _(sp):
            sp.dma_start(x_in[:], x[0]).then_inc(s_xin, 16)
            sp.wait_ge(s_set, 4)
            for dst, src in (
                (wt_theta[:, 0:IC], wT_theta), (wt_theta[:, IC:P], wT_theta),
                (wt_phi[:, 0:IC], wT_phi), (wt_phi[:, IC:P], wT_phi),
                (vec[0:IC, 0:1], b_theta), (vec[IC:P, 0:1], b_theta),
                (vec[0:IC, 1:2], b_phi), (vec[IC:P, 1:2], b_phi),
                (wt_g[:], wT_g), (g_bias[0:IC, 0:1], b_g), (wt_out[0:IC, :], wT_out),
                (wt_q[:], wT_q), (wk[:], w_k), (wt_v[:], wT_v), (idt[:], ident),
                (vec[:, 3:4], b_q), (vec[:, 4:5], b_k), (vec[:, 5:6], b_v),
            ):
                sp.dma_start(dst, src).then_inc(s_const, 16)
            sp.dma_start(vec[:, 7:8], b_out).then_inc(s_const, 16)

            def store(b, blk, parity):
                sp.wait_ge(s_done, b * (2 * BLOCKS) + BLOCKS + blk + 3)
                dst = out[b] if isinstance(b, int) else out[bass.ds(b, 1)].rearrange("a c n -> (a c) n")
                sp.dma_start(cols(dst, blk), result[:, parity]).then_inc(s_stored[parity], 16)

            def image(b, more):
                if more:
                    sp.wait_ge(s_done, b * (2 * BLOCKS) + BLOCKS + 2)
                    nxt = x[bass.ds(b + 1, 1)].rearrange("a c n -> (a c) n")
                    sp.dma_start(x_in[:], nxt).then_inc(s_xin, 16)
                with sp.Fori(0, BLOCKS // 2) as i:
                    store(b, 2 * i, 0)
                    store(b, 2 * i + 1, 1)

            with sp.Fori(0, B - 1) as b:
                image(b, True)
            image(B - 1, False)
            for parity in range(2):
                sp.wait_ge(s_stored[parity], 16 + 16 * B * BLOCKS // 2)

        @block.tensor
        def _(pe):
            mm = nc.tensor.matmul

            pe.wait_ge(s_const, 16 * CONSTS)
            pe.wait_ge(s_set, 8)
            mm(rough[:, 0:2], wk[:], ones[:, 0:2], start=True, stop=True)
            mm(rough[:, QB:QB + 2], wt_out[:], g_bias[:], start=True, stop=True).then_inc(s_small, 1)
            pe.wait_ge(s_vec, 1)

            def project(b, kind, c):
                n = CHUNK[kind, c]
                place = proj[:, n % BANKS]
                if n >= BANKS:
                    ready(pe, b, *chunk_list[n - BANKS])
                if kind in ("g", "v"):
                    src, w, per = (x_in, wt_g, G_PER_BANK) if kind == "g" else (x_mid, wt_v, V_PER_BANK)
                    for k in range(per):
                        tile, width = c * per + k, QB // per
                        last = mm(place[:, k * width:(k + 1) * width], src[:, tile * KT:(tile + 1) * KT],
                                  w[:], start=True, stop=True)
                else:
                    src, w = {"theta": (x_in, wt_theta), "phi": (x_in, wt_phi), "q": (x_mid, wt_q)}[kind]
                    last = mm(place, w[:], cols(src, c), start=True, stop=True)
                last.then_inc(s_proj, 1)

            def rough_piece(g, m, two_places=False):
                kk, t = divmod(m, SUB)
                if m == 0:
                    pe.wait_ge(s_stage, g + 1)
                pe.wait_ge(s_reduced, g * PIECES + m + (0 if two_places and m else 1))
                for h in range(TPG):
                    c = kk * GC + h * QB
                    place = acc_out[:, h] if two_places and m % 2 else rough[:, h * QB:(h + 1) * QB]
                    last = mm(place, q_stage[:, t * P:(t + 1) * P], keys_a[:, c:c + QB],
                              start=True, stop=True)
                last.then_inc(s_rough, 1)

            def shift_row(g, parity):
                pe.wait_ge(s_diag, g + 1)
                pe.wait_ge(s_done, g + 1)
                mm(acc_out[:, parity], ones_r[:], diag[:, parity], start=True, stop=True).then_inc(s_row, 1)

            def score_group(layer, g, blk, parity, s):
                pe.wait_ge(s_probs, (g * GROUPS + s) * 2 + 2)
                for h in range(TPG):
                    k = (s * TPG + h) * KT
                    place = scores[:, s % 2, h * QB:(h + 1) * QB]
                    mm(place, keys_a[:, k:k + KT], cols(qry_a, blk), start=True, stop=False)
                    if layer == 0:
                        last = mm(place, keys_b[:, k:k + KT], cols(qry_b, blk), start=False, stop=True)
                    else:
                        mm(place, keys_b[:, k:k + KT], cols(qry_a, blk), start=False, stop=False)
                        mm(place, keys_a[:, k:k + KT], cols(qry_b, blk), start=False, stop=False)
                        last = mm(place, ones_r[:], diag[:, parity], start=False, stop=True)
                last.then_inc(s_scores, 1)

            def value_group(layer, g, parity, s):
                if s == 0:
                    pe.wait_ge(s_done, g + 1)
                pe.wait_ge(s_split, g * GROUPS + s + 3)
                for h in range(TPG):
                    tile = s * TPG + h
                    hi = probs_hi[:, s % BUFS, h * QB:(h + 1) * QB]
                    lo = probs_lo[:, s % BUFS, h * QB:(h + 1) * QB]
                    o = acc_out[:, parity]
                    mm(o, values_hi(layer, tile), hi, start=tile == 0, stop=False)
                    mm(o, values_lo(layer, tile), hi, start=False, stop=False)
                    last = mm(o, values_hi(layer, tile), lo, start=False, stop=tile == TILES - 1)
                last.then_inc(s_used, 1)

            def denominators(layer, g, nth, parity):
                pe.wait_ge(s_y, g + 1)
                if layer == 1:
                    pe.wait_ge(s_fold, 3 * nth + 3)
                for t in range(SUB):
                    at = slice(t * P, (t + 1) * P)
                    part, pick = (y_sb[:, at], pick_den) if layer == 0 else (sums_pool[:, parity, at], ones)
                    last = mm(acc_out[:, parity, 2 * t:2 * t + 2], part, pick[:, 0:2], start=True, stop=True)
                last.then_inc(s_den, 1)

            def reciprocal_rows(g, parity):
                pe.wait_ge(s_rdiag, g + 1)
                mm(acc_out[:, parity], ones[:], rdiag[:], start=True, stop=True).then_inc(s_rden, 1)

            def out_projection(g, parity):
                pe.wait_ge(s_norm, g + 1)
                mm(acc_out[:, parity], wt_out[:], y_sb[:], start=True, stop=True).then_inc(s_wy, 1)

            with pe.Fori(0, B) as b:
                for layer in range(2):
                    g0 = b * (2 * BLOCKS) + layer * BLOCKS
                    pe.wait_ge(s_probs, g0 * (2 * GROUPS) + 4)
                    if layer == 0:
                        pe.wait_ge(s_xin, b * 16 + 16)
                    else:
                        pe.wait_ge(s_done, g0 + 2)
                    for kind, c in BETWEEN[layer]:
                        if kind == "piece":
                            m = c
                            if m == 1:
                                pe.wait_ge(s_done, g0 + 2)
                            if m % SUB == 0:
                                for h in range(TPG):
                                    ready(pe, b, ("phi", "k")[layer], m // SUB * TPG + h)
                            rough_piece(g0, m, two_places=True)
                        elif kind != "k":
                            project(b, kind, c)
                    if layer == 0:
                        shift_row(g0, 0)
                        pe.wait_ge(s_ones, b * 4 + 4)
                    pe.wait_ge(s_hi, b * len(HI) + (HI_L0, len(HI))[layer])
                    pe.wait_ge(s_lo, b * len(DVE_LO) + (DVE_L0, len(DVE_LO))[layer])
                    pe.wait_ge(s_plo, b * len(POOL_LO) + (POOL_L0, len(POOL_LO))[layer])

                    def blk_program(g, nth, blk, parity, first, last, layer=layer):
                        m = 0
                        for s in range(GROUPS):
                            if s == ROW_AT and layer == 0 and not last:
                                shift_row(g + 1, 1 - parity)
                            if s == 0 and layer == 0:
                                pe.wait_ge(s_row_sb, nth + 1)
                            if s == 0 and layer == 1:
                                pe.wait_ge(s_diag, g + 1)
                            score_group(layer, g, blk, parity, s)
                            if not last and PIECES_AT[s]:
                                rough_piece(g + 1, m)
                                m += 1
                            if not first and s == 4:
                                denominators(layer, g - 1, nth - 1, 1 - parity)
                            if not first and s == 6:
                                reciprocal_rows(g - 1, 1 - parity)
                            if not first and s == 8 and layer == 0:
                                out_projection(g - 1, 1 - parity)
                            if s >= LAG:
                                value_group(layer, g, parity, s - LAG)
                            elif not first:
                                value_group(layer, g - 1, 1 - parity, GROUPS + s - LAG)
                            if not last and PIECES_AT[s] == 2:
                                rough_piece(g + 1, m)
                                m += 1
                        if last:
                            for s in range(GROUPS - LAG, GROUPS):
                                value_group(layer, g, parity, s)
                            denominators(layer, g, nth, parity)
                            reciprocal_rows(g, parity)
                            if layer == 0:
                                out_projection(g, parity)

                    each_block(pe, b, layer, blk_program)

        @block.scalar
        def _(act):
            def copy(dst, src, bias=None, scale=1.0):
                if bias is None:
                    return nc.scalar.activation(dst, src, ACT.Copy)
                return nc.scalar.activation(dst, src, ACT.Identity, bias=bias, scale=scale)

            def take(b, kind, c):
                if kind == "k":
                    src, bias, scale = cols(x_mid, c), K_B, K_S
                else:
                    n = CHUNK[kind, c]
                    act.wait_ge(s_proj, b * ALL_CHUNKS + n + 1)
                    src, scale = proj[:, n % BANKS], 1.0
                    bias = {"theta": TH_B, "phi": PHI_B, "q": Q_B}.get(kind)
                if by_pool(kind, c):
                    w = WHOLE[kind, c]
                    if w >= 2:
                        act.wait_ge(s_plo, b * len(POOL_LO) + POOL_LO[kind, c] - 1)
                    copy(whole[:, w % 2], src, bias, scale)
                if kind == "phi":
                    copy(cols(keys_a[0:IC], c), src[0:IC], PHI_B[0:IC])
                    last = copy(cols(keys_b[IC:P], c), src[IC:P], PHI_B[IC:P])
                elif kind == "g":
                    last = copy(g_hi(c * G_PER_BANK, G_PER_BANK), src.rearrange("p (t c) -> p t c", c=IC))
                else:
                    dst = {"theta": qry_a, "q": qry_a, "k": keys_a, "v": vals}[kind]
                    last = copy(cols(dst, c), src, bias, scale)
                last.then_inc(s_hi, 1)

            def shift_to_row(nth, blk, parity):
                act.wait_ge(s_row, nth + 1)
                copy(cols(qry_b[0:IC], blk), acc_out[0:IC, parity]).then_inc(s_row_sb, 1)

            def take_output(layer, g, parity):
                act.wait_ge(s_used, (g + 1) * GROUPS + BUFS)
                act.wait_ge(s_done, g + 2)
                if layer == 0:
                    copy(y_sb[0:IC + 1], acc_out[0:IC + 1, parity]).then_inc(s_y, 1)
                else:
                    copy(o_sb[:], acc_out[:, parity]).then_inc(s_y, 1)

            def exponentials(layer, g, nth, s):
                n = g * GROUPS + s
                act.wait_ge(s_scores, n + 1)
                act.wait_ge(s_split, n + 1)
                if layer == 1:
                    before, blocks = (s - 2) % GROUPS, nth + (1 if s >= 2 else 0)
                    if before in POOL_ADDS:
                        act.wait_ge(s_plus, blocks * len(POOL_ADDS) + POOL_ADDS.index(before) + 1)
                    else:
                        act.wait_ge(s_added, blocks * len(DVE_ADDS) + DVE_ADDS.index(before) + 1)
                nc.scalar.activation(probs[:, s % 2], scores[:, s % 2], ACT.Exp,
                                     scale=SCALES[layer]).then_inc(s_probs, 1)
                act.wait_ge(s_used, n + 1)
                nc.scalar.activation(probs_hi[:, s % BUFS], scores[:, s % 2], ACT.Exp,
                                     scale=SCALES[layer]).then_inc(s_probs, 1)

            act.wait_ge(s_const, 16 * CONSTS)
            act.wait_ge(s_vec, 2)
            with act.Fori(0, B) as b:
                for layer in range(2):
                    g0 = b * (2 * BLOCKS) + layer * BLOCKS
                    act.wait_ge(s_used, g0 * GROUPS + BUFS)
                    if layer == 1:
                        act.wait_ge(s_done, g0 + 2)
                    for kind, c in BETWEEN[layer]:
                        if kind != "piece":
                            take(b, kind, c)
                    if layer == 0:
                        act.wait_ge(s_plo, b * len(POOL_LO) + POOL_L0)
                        shift_to_row(b * BLOCKS, 0, 0)
                    act.wait_ge(s_plo, b * len(POOL_LO) + (POOL_L0, len(POOL_LO))[layer])

                    def blk_program(g, nth, blk, parity, first, last, layer=layer):
                        for s in range(GROUPS):
                            if s == ROW_AT and layer == 0 and not last:
                                shift_to_row(nth + 1, blk + 1, 1 - parity)
                            if s == 2 and not first:
                                take_output(layer, g - 1, 1 - parity)
                            exponentials(layer, g, nth, s)
                        if last:
                            take_output(layer, g, parity)

                    each_block(act, b, layer, blk_program)

        @block.vector
        def _(dve):
            def piece(g, m, two_places=False):
                src = acc_out[:].rearrange("p h c -> p (h c)") if two_places and m % 2 else rough[:]
                kk, t = divmod(m, SUB)
                dve.wait_ge(s_rough, g * PIECES + m + 1)
                nc.vector.reduce_max(piece_max[:, t, kk:kk + 1], src, AX.X).then_inc(s_reduced, 1)

            def shift(g, parity):
                dve.wait_ge(s_reduced, (g + 1) * PIECES + 1)
                nc.vector.reduce_max(query_max[:], piece_max[:], AX.X).then_inc(s_qmax, 1)
                dve.wait_ge(s_qmax, g + 1)
                nc.vector.tensor_tensor(
                    diag[:, parity].rearrange("p (t c) -> p t c", c=P),
                    neg_ident[:].unsqueeze(1).to_broadcast([P, SUB, P]),
                    query_max[:].unsqueeze(2).to_broadcast([P, SUB, P]), ALU.mult).then_inc(s_diag, 1)

            def split(g, s):
                n = g * GROUPS + s
                dve.wait_ge(s_probs, 2 * n + 6)
                dve.wait_ge(s_used, n + 1)
                nc.vector.tensor_tensor(probs_lo[:, s % BUFS], probs[:, s % 2], rd(probs_hi[:, s % BUFS]),
                                        ALU.subtract).then_inc(s_split, 1)

            def add(nth, parity, s):
                if s not in DVE_ADDS:
                    return
                k = DVE_ADDS.index(s)
                if k == 0:
                    nc.vector.tensor_copy(sums[:, parity], probs[:, s % 2]).then_inc(s_added, 1)
                    return
                dve.wait_ge(s_added, (nth + 1) * len(DVE_ADDS) + k)
                nc.vector.tensor_tensor(sums[:, parity], sums[:, parity], probs[:, s % 2],
                                        ALU.add).then_inc(s_added, 1)

            def reciprocals(g, parity):
                dve.wait_ge(s_den, g + 1)
                den = acc_out[:, parity, 0:2 * SUB].rearrange("p (t c) -> p t c", c=2)[:, :, 0:1]
                nc.vector.reciprocal(rcol[:].unsqueeze(2), den).then_inc(s_rcol, 1)
                dve.wait_ge(s_rcol, g + 1)
                nc.vector.tensor_tensor(
                    rdiag[:].rearrange("p (t c) -> p t c", c=P), idt[:].unsqueeze(1).to_broadcast([P, SUB, P]),
                    rcol[:].unsqueeze(2).to_broadcast([P, SUB, P]), ALU.mult).then_inc(s_rdiag, 1)

            def normalise(layer, g, nth, parity):
                dve.wait_ge(s_rden, g + 1)
                if layer == 0:
                    nc.vector.tensor_tensor(y_sb[0:IC], y_sb[0:IC], acc_out[0:IC, parity],
                                            ALU.mult).then_inc(s_norm, 1)
                else:
                    dve.wait_ge(s_stored[parity], 8 * (nth - parity) + 16)
                    nc.vector.tensor_tensor(result[:, parity], o_sb[:], acc_out[:, parity],
                                            ALU.mult).then_inc(s_norm, 1)

            def finish(layer, g, nth, blk, parity):
                if layer == 0:
                    dve.wait_ge(s_wy, nth + 1)
                    src, dst, bias, before = acc_out[:, parity], cols(x_mid, blk), OUT_B, cols(x_in, blk)
                else:
                    dve.wait_ge(s_norm, g + 1)
                    src, dst, bias, before = result[:, parity], result[:, parity], V_B, cols(x_mid, blk)
                nc.vector.scalar_tensor_tensor(out=dst, in0=src, scalar=bias, in1=before,
                                               op0=ALU.add, op1=ALU.add).then_inc(s_done, 1)

            for free, n in ((s_reduced, 1), (s_probs, 4), (s_split, 2), (s_added, len(DVE_ADDS)),
                            (s_plus, len(POOL_ADDS)), (s_used, BUFS), (s_done, 2),
                            (s_stored[0], 16), (s_stored[1], 16)):
                dve.sem_inc(free, n)
            nc.vector.memset(ones[:], 1.0).then_inc(s_set, 1)
            nc.vector.memset(y_sb[:], 0.0).then_inc(s_set, 1)
            nc.vector.memset(g_bias[:], 0.0).then_inc(s_set, 1)
            nc.vector.memset(wt_out[:], 0.0).then_inc(s_set, 1)
            nc.vector.memset(pick_den[:], 0.0).then_inc(s_set, 1)
            dve.wait_ge(s_set, 5)
            nc.vector.memset(pick_den[IC:IC + 1, :], 1.0).then_inc(s_set, 1)
            nc.vector.tensor_copy(ones_r[:], ones[:]).then_inc(s_set, 1)
            dve.wait_ge(s_const, 16 * CONSTS)
            nc.vector.tensor_scalar(neg_ident[:], idt[:], -1.0, None, ALU.mult).then_inc(s_set, 1)
            dve.wait_ge(s_set, 8)
            dve.wait_ge(s_small, 1)
            nc.vector.tensor_copy(K_S, rough[:, 0:1]).then_inc(s_vec, 1)
            nc.vector.tensor_tensor(OUT_B, rough[:, QB:QB + 1], vec[:, 7:8], ALU.add).then_inc(s_vec, 1)
            dve.wait_ge(s_vec, 2)

            def lo_part(b, kind, c):
                ready(dve, b, kind, c, lo=False)
                rows = {"theta": slice(IC, P), "phi": slice(IC, P), "q": slice(0, P)}[kind]
                dst, bias, hi = {"theta": (qry_b, TH_B, qry_a), "phi": (keys_a, PHI_B, keys_b),
                                 "q": (qry_b, Q_B, qry_a)}[kind]
                nc.vector.scalar_tensor_tensor(
                    out=cols(dst[rows], c), in0=proj[rows, CHUNK[kind, c] % BANKS], scalar=bias[rows],
                    in1=rd(cols(hi[rows], c)), op0=ALU.add, op1=ALU.subtract).then_inc(s_lo, 1)

            with dve.Fori(0, B) as b:
                for layer in range(2):
                    g0 = b * (2 * BLOCKS) + layer * BLOCKS
                    for kind, c in BETWEEN[layer]:
                        if kind == "piece":
                            piece(g0, c, two_places=True)
                        elif (kind, c) in DVE_LO:
                            lo_part(b, kind, c)
                    shift(g0, 0)

                    def blk_program(g, nth, blk, parity, first, last, layer=layer):
                        m = 0
                        for s in range(GROUPS):
                            if s == DIAG_AT and not last:
                                shift(g + 1, 1 - parity)
                            if not last and PIECES_AT[s]:
                                piece(g + 1, m)
                                m += 1
                            if s > 0:
                                split(g, s - 1)
                                if layer == 1:
                                    add(nth, parity, s - 1)
                            elif not first:
                                split(g - 1, GROUPS - 1)
                                if layer == 1:
                                    add(nth - 1, 1 - parity, GROUPS - 1)
                            if not last and PIECES_AT[s] == 2:
                                piece(g + 1, m)
                                m += 1
                            if s == 5 and not first:
                                reciprocals(g - 1, 1 - parity)
                            if s == 7 and not first:
                                normalise(layer, g - 1, nth - 1, 1 - parity)
                            if s == (9 if layer == 0 else 7) and not first:
                                finish(layer, g - 1, nth - 1, blk - 1, 1 - parity)
                        if last:
                            split(g, GROUPS - 1)
                            if layer == 1:
                                add(nth, parity, GROUPS - 1)
                            reciprocals(g, parity)
                            normalise(layer, g, nth, parity)
                            finish(layer, g, nth, blk, parity)

                    each_block(dve, b, layer, blk_program)

        @block.gpsimd
        def _(pool):
            def settle():
                pool.sem_inc(s_settled, 1)

            def stage(g, blk):
                pool.wait_ge(s_reduced, g * PIECES + 1)
                settle()
                nc.gpsimd.tensor_copy(q_stage[:], rd(cols(qry_a, blk))).then_inc(s_stage, 1)

            def lo_part(b, kind, c):
                pool.wait_ge(s_hi, b * len(HI) + HI[kind, c] + 1)
                w = whole[:, WHOLE[kind, c] % 2]
                if kind == "g":
                    at = (c * G_PER_BANK, G_PER_BANK)
                    dst, hi, w = g_lo(*at), g_hi(*at), w.rearrange("p (t c) -> p t c", c=IC)
                elif kind == "v":
                    dst, hi = cols(vals[:, N:2 * N], c), cols(vals, c)
                else:
                    dst, hi = [cols(t, c) for t in ((keys_b, keys_a) if kind == "k" else (qry_b, qry_a))]
                nc.gpsimd.tensor_tensor(dst, w, rd(hi), ALU.subtract).then_inc(s_plo, 1)

            def fold(nth, parity):
                total = sums_pool[:, parity, 0:QB]
                pool.wait_ge(s_plus, (nth + 2) * len(POOL_ADDS))
                pool.wait_ge(s_added, (nth + 2) * len(DVE_ADDS))
                for k, part in enumerate((sums_pool[:, parity, QB:GC], sums[:, parity, 0:QB],
                                          sums[:, parity, QB:GC])):
                    if k:
                        pool.wait_ge(s_fold, 3 * nth + k)
                    nc.gpsimd.tensor_tensor(total, total, part, ALU.add).then_inc(s_fold, 1)

            def add(g, nth, parity, s):
                k = POOL_ADDS.index(s)
                pool.wait_ge(s_probs, (g * GROUPS + s) * 2 + 5)
                if k == 0:
                    pool.wait_ge(s_done, g + 1)
                    settle()
                    nc.gpsimd.tensor_copy(sums_pool[:, parity], probs[:, s % 2]).then_inc(s_plus, 1)
                    return
                pool.wait_ge(s_plus, (nth + 1) * len(POOL_ADDS) + k)
                nc.gpsimd.tensor_tensor(sums_pool[:, parity], sums_pool[:, parity], probs[:, s % 2],
                                        ALU.add).then_inc(s_plus, 1)

            with pool.Fori(0, B) as b:
                for layer in range(2):
                    g0 = b * (2 * BLOCKS) + layer * BLOCKS
                    pool.wait_ge(s_used, g0 * GROUPS + BUFS)
                    if layer == 0:
                        settle()
                        nc.gpsimd.memset(keys_b[0:IC, :].bitcast(F32), 1.0 / IC).then_inc(s_ones, 1)
                        tiles = vals[:, 0:TILES * VSTEP].bitcast(F32).rearrange("p (t c) -> p t c", c=VSTEP)
                        nc.gpsimd.memset(tiles[:, :, IC:IC + 1], 1.0).then_inc(s_ones, 1)
                        nc.gpsimd.memset(tiles[:, :, 2 * IC + 1:VSTEP], 0.0).then_inc(s_ones, 1)
                        nc.gpsimd.memset(vals[:, TILES * VSTEP:TILES * VSTEP + P].bitcast(F32), 0.0).then_inc(s_ones, 1)
                    ready(pool, b, ("theta", "q")[layer], 0, lo=False)
                    stage(g0, 0)
                    for kind, c in BETWEEN[layer]:
                        if (kind, c) in POOL_LO:
                            lo_part(b, kind, c)

                    def blk_program(g, nth, blk, parity, first, last, layer=layer):
                        if not last:
                            stage(g + 1, blk + 1)
                        if layer == 1:
                            if not first:
                                fold(nth - 1, 1 - parity)
                            for s in POOL_ADDS:
                                add(g, nth, parity, s)
                            if last:
                                fold(nth, parity)

                    each_block(pool, b, layer, blk_program)


def kernel(x, L0_conv_g_w, L0_conv_g_b, L0_conv_theta_w, L0_conv_theta_b, L0_conv_phi_w, L0_conv_phi_b,
           L0_conv_W_w, L0_conv_W_b, L1_conv_Wq, L1_conv_bq, L1_conv_Wk, L1_conv_bk, L1_conv_Wv, L1_conv_bv):
    import numpy as np
    import concourse.bacc as bacc
    from concourse.bass_utils import run_bass_kernel_spmd

    def turned(w):
        return np.ascontiguousarray(np.asarray(w).T)

    def column(v):
        return np.asarray(v).reshape(-1, 1)

    shape = np.shape(x)
    arrays = {
        "x": np.ascontiguousarray(np.asarray(x).reshape(shape[0], shape[1], -1)),
        "wT_theta": turned(L0_conv_theta_w), "b_theta": column(L0_conv_theta_b),
        "wT_phi": turned(L0_conv_phi_w), "b_phi": column(L0_conv_phi_b),
        "wT_g": turned(L0_conv_g_w), "b_g": column(L0_conv_g_b),
        "wT_out": turned(L0_conv_W_w), "b_out": column(L0_conv_W_b),
        "wT_q": turned(L1_conv_Wq), "b_q": column(L1_conv_bq),
        "w_k": np.asarray(L1_conv_Wk), "b_k": column(L1_conv_bk),
        "wT_v": turned(L1_conv_Wv), "b_v": column(L1_conv_bv),
        "ident": np.eye(P, dtype=np.float32),
    }
    nc = bacc.Bacc("TRN2", target_bir_lowering=False, num_devices=1)
    args = {n: nc.dram_tensor(n, a.shape, mybir.dt.from_np(a.dtype), kind="ExternalInput").ap()
            for n, a in arrays.items()}
    out = nc.dram_tensor("out", arrays["x"].shape, F32, kind="ExternalOutput").ap()
    build(nc, out=out, **args)
    r = run_bass_kernel_spmd(nc, [arrays], core_ids=[0])
    return r.results[0]["out"].reshape(shape)
```

```python
from contextlib import ExitStack

import concourse.bass as bass
from concourse import mybir

ALU = mybir.AluOpType
ACT = mybir.ActivationFunctionType
AX = mybir.AxisListType
F32 = mybir.dt.float32
F32R = mybir.dt.float32r

P = 128
QB = 512
KT = 128
TPG = 2
GC = TPG * QB
SUB = QB // P
HI_BUFS, LO_BUFS = 4, 4
LAG = 3

PIECES_AT = [[3 if s in three else 2 if s < 14 else 0 for s in range(16)]
             for three in ((7, 8, 11, 13), (7, 8, 10, 12))]
TURN_PIECES_AT = [2] * 14 + [0, 0]
TAKE_AT = 3
FOLD_AT = 1
DEN_AT = 5
RDEN_AT = 8
OUT_AT = 10
FINISH_AT = (11, 9)
PHI_AT, G_AT = 9, 11
K_AT, V_AT = 11, 11
NEXT_Q_AT = 14
Q_LO_AT = 5
DIAG_AT = 14
ROW_AT = 15
K_LO_AT, V_LO_AT = 12, 14

SHIFTED = (1, 3, 4, 6, 9, 11, 13, 14, 15)


class Step:

    def __init__(self, layer, b, i, i_known, prev, nxt, more, blocks, pieces_per_block):
        self.layer, self.b, self.i, self.prev, self.nxt = layer, b, i, prev, nxt
        self.parity = i_known % 2
        self.g = b * (2 * blocks) + layer * blocks + i
        self.nth = b * blocks + i
        self.turn = nxt == 1 and layer == 0
        self.ends = self.turn or nxt is None
        self.pieces = (self.g + 1) * pieces_per_block
        self.next_q = None
        if i_known < blocks - 2:
            self.next_q = (layer, b, i + 2)
        elif more and layer == 1:
            self.next_q = (0, b + 1, i_known + 2 - blocks)
        elif i_known == blocks - 2 and layer == 0:
            self.next_q = (1, b, 0)
        self.kv = layer == 0 and i_known > 0
        self.phi_g = layer == 1 and more


def build(nc, x, wT_theta, b_theta, wT_phi, b_phi, wT_g, b_g, wT_out, b_out,
          wT_q, b_q, w_k, b_k, wT_v, b_v, ident, out):
    B, C, N = x.shape
    IC = wT_theta.shape[1]
    assert C == P and 2 * IC == P and N % (2 * QB) == 0
    BLOCKS = N // QB
    TILES = N // KT
    GROUPS = TILES // TPG
    PIECES = SUB * BLOCKS
    assert all(GROUPS == len(a) and sum(a) == PIECES for a in PIECES_AT) and PIECES == sum(TURN_PIECES_AT) + SUB
    assert BLOCKS == 8 and LAG == 3
    ADDS = GROUPS - 1
    TPC = QB // KT
    SCALES = (1.0, float(C) ** -0.5)
    CONSTS = 20

    pieces = [(t, c) for c in range(BLOCKS) for t in range(SUB)]
    last_pieces = pieces[-SUB:]

    with ExitStack() as ctx:
        def sb(name, shape, dt=F32):
            return ctx.enter_context(nc.sbuf_tensor(name, shape, dt))

        def sem(name):
            return ctx.enter_context(nc.semaphore(name))

        mid = nc.dram_tensor("mid", [B, C, N], F32, kind="Internal").ap()

        scores = ctx.enter_context(nc.psum_tensor("scores", [P, 2, GC], F32))
        rough = ctx.enter_context(nc.psum_tensor("rough", [P, GC], F32))
        acc_out = ctx.enter_context(nc.psum_tensor("acc_out", [P, 2, QB], F32))

        phi_a = sb("phi_a", [P, N], F32R)
        phi_b = sb("phi_b", [P, N], F32R)
        k_hi = sb("k_hi", [P, N], F32R)
        k_lo = sb("k_lo", [P, N], F32R)
        g_vals = sb("g_vals", [P, N], F32R)
        v_vals = sb("v_vals", [P, 2 * N], F32R)
        mid_new = sb("mid_new", [P, 2, QB])
        x_kv = sb("x_kv", [P, QB])
        x_q = sb("x_q", [P, QB])
        x_res = sb("x_res", [P, QB])
        qry_a = sb("qry_a", [P, 2, QB], F32R)
        q_whole = sb("q_whole", [P, QB])
        qry_b = sb("qry_b", [P, 2, QB], F32R)
        whole = sb("whole", [P, 2, QB])
        probs = sb("probs", [P, 2, GC])
        probs_hi = sb("probs_hi", [P, HI_BUFS, GC], F32R)
        probs_lo = sb("probs_lo", [P, LO_BUFS, GC], F32R)
        diag = sb("diag", [P, 2, QB], F32R)
        piece_max = sb("piece_max", [P, SUB, BLOCKS])
        query_max = sb("query_max", [P, SUB])
        sums = sb("sums", [P, 2, GC])
        shift_rows = sb("shift_rows", [P, 2, QB])
        total = sb("total", [P, QB])
        o_sb = sb("o_sb", [P, QB])
        rcol = sb("rcol", [P, SUB])
        rparts = sb("rparts", [P, 2, SUB], F32R)
        rdiag = sb("rdiag", [P, 2, QB], F32R)
        result = sb("result", [P, QB])
        wt_theta = sb("wt_theta", [P, P])
        wt_phi = sb("wt_phi", [P, P])
        wt_g = sb("wt_g", [P, IC])
        wt_out = sb("wt_out", [P, C])
        wt_q = sb("wt_q", [P, C])
        wk = sb("wk", [P, C])
        wt_v = sb("wt_v", [P, C])
        neg_ident = sb("neg_ident", [P, P])
        idt = sb("idt", [P, P])
        ones = sb("ones", [P, P])
        ones_r = sb("ones_r", [P, P], F32R)
        vec = sb("vec", [P, 8])
        TH_B, PHI_B, OUT_B, Q_B, K_B, V_B, K_S = (vec[:, i:i + 1] for i in range(7))
        g_bias = sb("g_bias", [P, 2])

        def first_image(c):
            place = probs if c < BLOCKS // 2 else sums
            return place[:].rearrange("p a (h c) -> p (a h) c", c=QB)[:, c % (BLOCKS // 2)]

        s_const = sem("s_const")
        s_set = sem("s_set")
        s_ones = sem("s_ones")
        s_small = sem("s_small")
        s_vec = sem("s_vec")
        s_x0 = sem("s_x0")
        s_xkv = sem("s_xkv")
        s_xq = sem("s_xq")
        s_xres = sem("s_xres")
        p_q, h_q, l_q = sem("p_q"), sem("h_q"), sem("l_q")
        p_phi, h_phi, l_phi = sem("p_phi"), sem("h_phi"), sem("l_phi")
        p_g, h_g, l_g = sem("p_g"), sem("h_g"), sem("l_g")
        h_k, l_k = sem("h_k"), sem("l_k")
        s_k_hi = sem("s_k_hi")
        p_v, h_v, l_v = sem("p_v"), sem("h_v"), sem("l_v")
        s_settled = {nc.gpsimd: sem("s_settled_pool"), nc.sync: sem("s_settled_sp")}
        s_rough = sem("s_rough")
        s_reduced = sem("s_reduced")
        s_qmax = sem("s_qmax")
        s_diag = sem("s_diag")
        s_row = sem("s_row")
        s_row_sb = sem("s_row_sb")
        s_shifted = sem("s_shifted")
        s_scores = sem("s_scores")
        s_probs = sem("s_probs")
        s_split = sem("s_split")
        s_plus = sem("s_plus")
        s_used = sem("s_used")
        s_y = sem("s_y")
        s_fold = sem("s_fold")
        s_den = sem("s_den")
        s_rcol = sem("s_rcol")
        s_rparts = sem("s_rparts")
        s_rdiag = sem("s_rdiag")
        s_rden = sem("s_rden")
        s_wy = sem("s_wy")
        s_norm = sem("s_norm")
        s_done = sem("s_done")
        s_mid = sem("s_mid")
        s_stored = sem("s_stored")

        def cols(t, i, n=QB):
            return t[:, bass.ds(i * n, n)] if not isinstance(i, int) else t[:, i * n:(i + 1) * n]

        def image(t, b):
            return t[b] if isinstance(b, int) else t[bass.ds(b, 1)].rearrange("a c n -> (a c) n")

        def settle(eng):
            eng.sem_inc(s_settled[eng], 1)

        def rd(ap):
            return ap.bitcast(F32)

        def g_part(c, lo):
            at = cols(g_vals, c).rearrange("p (t c) -> p t c", c=P)
            return at[:, :, IC:P] if lo else at[:, :, 0:IC]

        def run_layer(eng, b, layer, prev, more, block):
            def step(i, i_known):
                nxt = layer if i_known < BLOCKS - 1 else (1 if layer == 0 else 0 if more else None)
                st = Step(layer, b, i, i_known, layer if i_known else prev, nxt, more,
                          BLOCKS, PIECES)
                block(st)

            step(0, 0)
            with eng.Fori(0, 2) as j:
                step(2 * j + 1, 1)
                step(2 * j + 2, 2)
            for i in range(5, BLOCKS):
                step(i, i)

        def run_all(eng, turn, block):
            run_layer(eng, 0, 0, None, True, block)
            with eng.Fori(0, B - 1) as b:
                turn(b)
                run_layer(eng, b, 1, None, True, block)
                run_layer(eng, b + 1, 0, 1, True, block)
            turn(B - 1)
            run_layer(eng, B - 1, 1, None, False, block)

        def added(g, s):
            return g * ADDS + max(s, 1) + 2

        def shifted(nth, s):
            return nth * len(SHIFTED) + SHIFTED.index(s) + 1

        def fold(eng, g, parity):
            eng.wait_ge(s_plus, added(g, GROUPS - 1))
            eng.wait_ge(s_den, g + 1)
            eng.tensor_tensor(total[:], sums[:, parity, 0:QB], sums[:, parity, QB:GC],
                              ALU.add).then_inc(s_fold, 1)

        def add(eng, layer, g, parity, s):
            if s == 0:
                return
            eng.wait_ge(s_probs, (g * GROUPS + s) * 2 + (6 if layer == 1 and s in SHIFTED else 5))
            if s == 1:
                eng.tensor_tensor(sums[:, parity], probs[:, 0], probs[:, 1], ALU.add).then_inc(s_plus, 1)
                return
            eng.wait_ge(s_plus, added(g, s - 1))
            eng.tensor_tensor(sums[:, parity], sums[:, parity], probs[:, s % 2],
                              ALU.add).then_inc(s_plus, 1)

        def before(st):
            nth = st.nth - 1
            return st.prev, st.g - 1, nth, 1 - st.parity

        def end_of_layer0(b):
            return 0, b * (2 * BLOCKS) + BLOCKS - 1, b * BLOCKS + BLOCKS - 1, 1

        def two_banks(m):
            return cols(rough, m % 2)

        four_banks = (rough[:, 0:QB], rough[:, QB:GC], acc_out[:, 0], acc_out[:, 1])

        block = ctx.enter_context(nc.Block())

        @block.sync
        def _(sp):
            for h, place in enumerate((probs, sums)):
                sp.dma_start(place[:].rearrange("p a c -> p (a c)"),
                             x[0][:, h * (N // 2):(h + 1) * (N // 2)]).then_inc(s_x0, 16)
            sp.wait_ge(s_set, 2)
            for dst, src in (
                (wt_phi[:, 0:IC], wT_phi), (wt_phi[:, IC:P], wT_phi),
                (vec[0:IC, 1:2], b_phi), (vec[IC:P, 1:2], b_phi), (wt_g[:], wT_g),
                (wt_theta[:, 0:IC], wT_theta), (wt_theta[:, IC:P], wT_theta),
                (vec[0:IC, 0:1], b_theta), (vec[IC:P, 0:1], b_theta), (idt[:], ident),
                (g_bias[0:IC, 0:1], b_g), (wt_out[0:IC, :], wT_out), (wt_out[IC:P, :], wT_out), (vec[:, 7:8], b_out),
                (wt_q[:], wT_q), (wk[:], w_k), (wt_v[:], wT_v),
                (vec[:, 3:4], b_q), (vec[:, 4:5], b_k), (vec[:, 5:6], b_v),
            ):
                sp.dma_start(dst, src).then_inc(s_const, 16)

            def load_q(g, layer, b, i):
                sp.wait_ge(p_q, g)
                if layer == 1:
                    sp.wait_ge(s_mid, (b * BLOCKS + i) * 16 + 48)
                settle(sp)
                sp.dma_start(x_q[:], cols(image((x, mid)[layer], b), i)).then_inc(s_xq, 16)

            def load_residual(g, layer, b, i):
                sp.wait_ge(s_done, g + 2)
                settle(sp)
                sp.dma_start(x_res[:], cols(image((x, mid)[layer], b), i)).then_inc(s_xres, 16)

            def store_mid(b, i, parity):
                settle(sp)
                sp.dma_start(cols(image(mid, b), i), mid_new[:, parity]).then_inc(s_mid, 16)

            def store_out(b, i):
                settle(sp)
                sp.dma_start(cols(image(out, b), i), result[:]).then_inc(s_stored, 16)

            def block_program(st):
                if st.phi_g:
                    sp.wait_ge(p_phi, (st.b + 1) * BLOCKS + st.i)
                    sp.wait_ge(p_g, (st.b + 1) * BLOCKS + st.i)
                    settle(sp)
                    sp.dma_start(x_kv[:], cols(image(x, st.b + 1), st.i)).then_inc(s_xkv, 16)
                if st.next_q:
                    load_q(st.g + 2, *st.next_q)
                if st.prev is not None:
                    sp.wait_ge(s_done, st.g + 2)
                    if st.prev != st.layer:
                        store_out(st.b - 1, BLOCKS - 1)
                    elif st.prev == 1:
                        store_out(st.b, st.i - 1)
                    else:
                        store_mid(st.b, st.i - 1, 1 - st.parity)
                load_residual(st.g, st.layer, st.b, st.i)

            def turn(b):
                _, g, _, parity = end_of_layer0(b)
                load_q(g + 2, 1, b, 1)
                sp.wait_ge(s_done, g + 3)
                store_mid(b, BLOCKS - 1, parity)

            load_q_first = sp.dma_start(x_q[:], cols(image(x, 0), 0))
            load_q_first.then_inc(s_xq, 16)
            load_q(1, 0, 0, 1)
            run_all(sp, turn, block_program)
            sp.wait_ge(s_done, 2 * B * BLOCKS + 2)
            store_out(B - 1, BLOCKS - 1)
            sp.wait_ge(s_stored, 16 * B * BLOCKS + 16)
            sp.wait_ge(s_mid, 16 * B * BLOCKS + 32)

        @block.tensor
        def _(pe):
            mm = nc.tensor.matmul

            def project(place, w, src, done):
                mm(place, w[:], src, start=True, stop=True).then_inc(done, 1)

            def project_keys(place, w, src, done):
                width = w.shape[1]
                for k in range(TPC):
                    last = mm(place[:, k * width:(k + 1) * width], src[:, k * KT:(k + 1) * KT], w[:],
                              start=True, stop=True)
                last.then_inc(done, 1)

            def next_queries(g, layer, place):
                pe.wait_ge(s_xq, 16 * g + 16)
                project(place, (wt_theta, wt_q)[layer], x_q[:], p_q)

            def rough_piece(layer, parity, piece, place):
                t, c = piece
                keys = (phi_a, k_hi)[layer]
                mm(place, qry_a[:, parity, t * P:(t + 1) * P], cols(keys, c), start=True, stop=True).then_inc(s_rough, 1)

            def shift_row(g, parity):
                pe.wait_ge(s_diag, g + 1)
                pe.wait_ge(s_done, g + 1)
                mm(acc_out[:, parity], ones_r[:], diag[:, parity], start=True, stop=True).then_inc(s_row, 1)

            def score_group(layer, prev, g, nth, parity, s):
                if layer == 1 and s - 2 in SHIFTED:
                    pe.wait_ge(s_shifted, shifted(nth, s - 2))
                elif s < 2 and prev == 1:
                    pe.wait_ge(s_shifted, shifted(nth - 1, GROUPS + s - 2))
                else:
                    pe.wait_ge(s_probs, (g * GROUPS + s) * 2 + 2)
                qa, qb = qry_a[:, parity], qry_b[:, parity]
                for h in range(TPG):
                    k = slice((s * TPG + h) * KT, (s * TPG + h + 1) * KT)
                    place = scores[:, s % 2, h * QB:(h + 1) * QB]
                    if layer == 0:
                        mm(place, phi_a[:, k], qa, start=True, stop=False)
                        if s == 0 and h == 0:
                            pe.wait_ge(s_row_sb, g + 1)
                        last = mm(place, phi_b[:, k], qb, start=False, stop=True)
                    else:
                        mm(place, k_hi[:, k], qa, start=True, stop=False)
                        mm(place, k_lo[:, k], qa, start=False, stop=False)
                        if s == 0 and h == 0:
                            pe.wait_ge(l_q, g + 1)
                        last = mm(place, k_hi[:, k], qb, start=False, stop=s in SHIFTED)
                        if s == 0 and h == 0:
                            pe.wait_ge(s_diag, g + 1)
                        if s not in SHIFTED:
                            last = mm(place, ones_r[:], diag[:, parity], start=False, stop=True)
                last.then_inc(s_scores, 1)

            def value_group(layer, g, parity, s):
                if s == 0:
                    pe.wait_ge(s_done, g + 1)
                    pe.wait_ge(s_row_sb, g + 1)
                pe.wait_ge(s_split, g * GROUPS + s + 3)
                for h in range(TPG):
                    tile = s * TPG + h
                    hi = probs_hi[:, s % HI_BUFS, h * QB:(h + 1) * QB]
                    lo = probs_lo[:, s % LO_BUFS, h * QB:(h + 1) * QB]
                    o, first, end = acc_out[:, parity], tile == 0, tile == TILES - 1
                    if layer == 0:
                        g_tile = cols(g_vals, tile, P)
                        mm(o, g_tile, hi, start=first, stop=False)
                        last = mm(o, g_tile, lo, start=False, stop=end)
                    else:
                        v_hi, v_lo = cols(v_vals[:, 0:N], tile, P), cols(v_vals[:, N:2 * N], tile, P)
                        mm(o, v_hi, hi, start=first, stop=False)
                        mm(o, v_lo, hi, start=False, stop=False)
                        last = mm(o, v_hi, lo, start=False, stop=end)
                last.then_inc(s_used, 1)

            def denominators(g, parity):
                pe.wait_ge(s_y, g + 1)
                pe.wait_ge(s_fold, g + 1)
                for t in range(SUB):
                    last = mm(acc_out[:, parity, 2 * t:2 * t + 2], total[:, t * P:(t + 1) * P], ones[:, 0:2],
                              start=True, stop=True)
                last.then_inc(s_den, 1)

            def reciprocal_rows(g, parity):
                pe.wait_ge(s_rdiag, 2 * g + 2)
                mm(acc_out[:, parity], ones_r[:], rdiag[:, 0], start=True, stop=False)
                mm(acc_out[:, parity], ones_r[:], rdiag[:, 1], start=False, stop=True).then_inc(s_rden, 1)

            def out_projection(g, parity):
                pe.wait_ge(s_norm, g + 1)
                mm(acc_out[:, parity], wt_out[:], o_sb[:], start=True, stop=True).then_inc(s_wy, 1)

            pe.wait_ge(s_const, 16 * CONSTS)
            pe.wait_ge(s_set, 4)
            mm(rough[:, 0:2], wk[:], ones[:, 0:2], start=True, stop=True)
            mm(rough[:, QB:QB + 2], wt_out[:], g_bias[:], start=True, stop=True).then_inc(s_small, 1)
            pe.wait_ge(s_x0, 32)
            pe.wait_ge(s_vec, 2)
            next_queries(0, 0, rough[:, 0:QB])

            def first_pieces(c):
                if c == 0:
                    pe.wait_ge(h_q, 1)
                pe.wait_ge(l_phi, c + 2)
                for m in range(c * SUB, (c + 1) * SUB):
                    if m >= SUB:
                        pe.wait_ge(s_reduced, m - SUB + 2)
                    rough_piece(0, 0, pieces[m], four_banks[m % SUB])

            for c in range(BLOCKS):
                if c >= 2:
                    pe.wait_ge(h_phi, c - 1)
                    pe.wait_ge(h_g, c - 1)
                project(scores[:, c % 2, 0:QB], wt_phi, first_image(c), p_phi)
                project_keys(scores[:, c % 2, QB:GC], wt_g, first_image(c), p_g)
                if c > 0:
                    first_pieces(c - 1)
            first_pieces(BLOCKS - 1)
            shift_row(0, 0)
            pe.wait_ge(s_reduced, PIECES + 1)
            next_queries(1, 0, rough[:, 0:QB])
            pe.wait_ge(s_ones, 1)
            pe.wait_ge(h_g, BLOCKS)
            pe.wait_ge(l_g, BLOCKS + 1)

            def block_program(st):
                at = TURN_PIECES_AT if st.turn else PIECES_AT[st.layer]
                free_bank = acc_out[:, 1 - st.parity]
                m = 0

                def piece():
                    nonlocal m
                    t, c = pieces[m]
                    if m == 0:
                        pe.wait_ge(h_q, st.g + 2)
                    if t == 0 and st.turn:
                        pe.wait_ge(s_k_hi, st.b * BLOCKS + c + 1)
                    if t == 0 and st.layer == 1 and st.nxt == 0:
                        pe.wait_ge(l_phi, (st.b + 1) * BLOCKS + c + 2)
                    pe.wait_ge(s_reduced, st.pieces + m)
                    rough_piece(st.nxt, 1 - st.parity, pieces[m], two_banks(m))
                    m += 1

                for s in range(GROUPS):
                    if s == ROW_AT and st.nxt is not None and not st.turn:
                        if st.kv:
                            pe.wait_ge(h_v, st.nth)
                        if st.phi_g:
                            pe.wait_ge(h_g, (st.b + 1) * BLOCKS + st.i + 1)
                        shift_row(st.g + 1, 1 - st.parity)
                    if st.layer == 1 and st.prev is None:
                        if s == 1:
                            pe.wait_ge(h_q, st.g + 2)
                            pe.wait_ge(h_v, (st.b + 1) * BLOCKS)
                        if s == GROUPS - TPC // TPG:
                            pe.wait_ge(l_k, (st.b + 1) * BLOCKS + 1)
                            pe.wait_ge(l_v, (st.b + 1) * BLOCKS + 1)
                    if s == 0 and st.layer == 0 and st.prev == 1:
                        pe.wait_ge(l_g, (st.b + 1) * BLOCKS + 1)
                    score_group(st.layer, st.prev, st.g, st.nth, st.parity, s)
                    if st.nxt is not None:
                        for _ in range(min(at[s], 2)):
                            piece()
                    if s == 0 and st.layer == 1 and st.prev is None:
                        shift_row(st.g, st.parity)
                    if st.prev is not None:
                        layer, g, nth, parity = before(st)
                        if s == DEN_AT:
                            denominators(g, parity)
                        if s == OUT_AT and layer == 0:
                            out_projection(g, parity)
                    if s >= LAG:
                        value_group(st.layer, st.g, st.parity, s - LAG)
                    elif st.prev is not None:
                        value_group(st.prev, st.g - 1, 1 - st.parity, GROUPS + s - LAG)
                    if s == RDEN_AT and st.prev is not None:
                        reciprocal_rows(st.g - 1, 1 - st.parity)
                    if st.nxt is not None and at[s] == 3:
                        piece()
                    if s == PHI_AT and st.phi_g:
                        n = (st.b + 1) * BLOCKS + st.i
                        pe.wait_ge(s_xkv, 16 * (n - BLOCKS) + 16)
                        pe.wait_ge(s_done, st.g + 2)
                        project(free_bank, wt_phi, x_kv[:], p_phi)
                    if s == G_AT and st.phi_g:
                        pe.wait_ge(h_phi, (st.b + 1) * BLOCKS + st.i + 1)
                        project_keys(free_bank, wt_g, x_kv[:], p_g)
                    if s == V_AT and st.kv:
                        pe.wait_ge(s_done, st.g + 2)
                        project_keys(free_bank, wt_v, mid_new[:, 1 - st.parity], p_v)
                    if s == NEXT_Q_AT and st.next_q:
                        pe.wait_ge(s_reduced, st.pieces + PIECES + 1)
                        next_queries(st.g + 2, st.next_q[0], two_banks(1))
                if st.ends:
                    for s in range(GROUPS - LAG, GROUPS):
                        value_group(st.layer, st.g, st.parity, s)
                    if st.turn:
                        pe.wait_ge(s_probs, (st.g + 1) * (2 * GROUPS) + 4)
                        next_queries(st.g + 2, 1, scores[:, 1, 0:QB])
                    denominators(st.g, st.parity)
                    reciprocal_rows(st.g, st.parity)
                    if st.layer == 0:
                        out_projection(st.g, st.parity)

            def turn(b):
                _, g, nth, parity = end_of_layer0(b)
                pe.wait_ge(s_done, g + 3)
                pe.wait_ge(s_k_hi, nth + 1)
                pe.wait_ge(s_reduced, (g + 2) * PIECES - SUB + 1)
                for t, piece in enumerate(last_pieces):
                    rough_piece(1, 1 - parity, piece, four_banks[t])
                project_keys(scores[:, 1, QB:GC], wt_v, mid_new[:, parity], p_v)

            run_all(pe, turn, block_program)

        @block.scalar
        def _(act):
            def copy(dst, src, bias=None, scale=1.0):
                if bias is None:
                    return nc.scalar.activation(dst, src, ACT.Copy)
                return nc.scalar.activation(dst, src, ACT.Identity, bias=bias, scale=scale)

            def scaled(dst, src, scale):
                return nc.scalar.activation(dst, src[:], ACT.Copy, scale=scale)

            def take_q_whole(g, layer, src):
                act.wait_ge(p_q, g + 1)
                if not (isinstance(g, int) and g == 0):
                    act.wait_ge(l_q, g)
                copy(q_whole[:], src, (TH_B, Q_B)[layer])

            def take_q_hi(layer, parity, src):
                copy(qry_a[:, parity], src, (TH_B, Q_B)[layer]).then_inc(h_q, 1)

            def take_phi(n, c, src):
                act.wait_ge(p_phi, n + 1)
                act.wait_ge(l_phi, n + 1)
                copy(whole[0:IC, 0], src[0:IC], PHI_B[0:IC])
                copy(cols(phi_b, c)[IC:P], src[IC:P], PHI_B[IC:P])
                copy(cols(phi_a, c), src, PHI_B).then_inc(h_phi, 1)

            def take_g(n, c, src):
                act.wait_ge(p_g, n + 1)
                act.wait_ge(l_g, n + 1)
                src = src[:, 0:TPC * IC]
                copy(whole[:, 1, 0:TPC * IC], src)
                copy(g_part(c, False), src.rearrange("p (t c) -> p t c", c=IC)).then_inc(h_g, 1)

            def make_k(n, c, src):
                act.wait_ge(l_k, n + 1)
                copy(cols(k_hi, c), src, K_B, K_S).then_inc(s_k_hi, 1)
                copy(whole[:, 0], src, K_B, K_S).then_inc(h_k, 1)

            def take_v(n, c, src):
                act.wait_ge(p_v, n + 1)
                act.wait_ge(l_v, n + 1)
                copy(whole[:, 1], src)
                copy(cols(v_vals, c), src).then_inc(h_v, 1)

            def shift_to_row(layer, g, parity):
                act.wait_ge(s_row, g + 1)
                if layer == 0:
                    act.wait_ge(l_q, g + 1)
                    copy(qry_b[0:IC, parity], acc_out[0:IC, parity]).then_inc(s_row_sb, 1)
                else:
                    copy(shift_rows[:, parity], acc_out[:, parity]).then_inc(s_row_sb, 1)

            def reciprocal_diag(g, part):
                act.wait_ge(s_rparts, 2 * g + part + 1)
                for t in range(SUB):
                    last = scaled(rdiag[:, part, t * P:(t + 1) * P], idt, rd(rparts[:, part, t:t + 1]))
                last.then_inc(s_rdiag, 1)

            def take_output(g, parity):
                act.wait_ge(s_used, (g + 1) * GROUPS + HI_BUFS)
                act.wait_ge(s_done, g + 2)
                copy(o_sb[:], acc_out[:, parity]).then_inc(s_y, 1)

            def probs_shifted(g, nth, s):
                act.wait_ge(s_shifted, shifted(nth, s))
                act.wait_ge(s_used, g * GROUPS + s + 1)
                for dst in (probs_hi[:, s % HI_BUFS], probs[:, s % 2]):
                    nc.scalar.activation(dst, probs[:, s % 2], ACT.Exp, scale=SCALES[1]).then_inc(s_probs, 1)

            def probs_whole(layer, g, s):
                n = g * GROUPS + s
                act.wait_ge(s_scores, n + 1)
                act.wait_ge(s_split, n + 1)
                act.wait_ge(s_plus, added(g, s - 2) if s >= 2 else g * ADDS + s + 1)
                nc.scalar.activation(probs[:, s % 2], scores[:, s % 2], ACT.Exp,
                                     scale=SCALES[layer]).then_inc(s_probs, 1)

            def probs_rounded(layer, g, s):
                act.wait_ge(s_used, g * GROUPS + s + 1)
                nc.scalar.activation(probs_hi[:, s % HI_BUFS], scores[:, s % 2], ACT.Exp,
                                     scale=SCALES[layer]).then_inc(s_probs, 1)

            act.wait_ge(s_const, 16 * CONSTS)
            act.wait_ge(s_vec, 2)
            take_q_whole(0, 0, rough[:, 0:QB])
            take_q_hi(0, 0, rough[:, 0:QB])
            for c in range(BLOCKS):
                take_phi(c, c, scores[:, c % 2, 0:QB])
                take_g(c, c, scores[:, c % 2, QB:GC])
            shift_to_row(0, 0, 0)
            take_q_whole(1, 0, rough[:, 0:QB])
            take_q_hi(0, 1, rough[:, 0:QB])

            def block_program(st):
                free_bank = acc_out[:, 1 - st.parity]
                for s in range(GROUPS):
                    if s == GROUPS - 1 and st.next_q:
                        take_q_whole(st.g + 2, st.next_q[0], two_banks(1))
                    if s == ROW_AT and st.nxt is not None and not st.turn:
                        shift_to_row(st.nxt, st.g + 1, 1 - st.parity)
                    if s == TAKE_AT and st.prev is not None:
                        layer, g, _, parity = before(st)
                        take_output(g, parity)
                    if st.layer == 1 and s in SHIFTED:
                        if s == GROUPS - 1 and st.next_q:
                            act.wait_ge(s_scores, (st.g + 1) * GROUPS)
                            take_q_hi(st.next_q[0], st.parity, two_banks(1))
                        probs_shifted(st.g, st.nth, s)
                    else:
                        probs_whole(st.layer, st.g, s)
                        if s == GROUPS - 1 and st.next_q:
                            take_q_hi(st.next_q[0], st.parity, two_banks(1))
                        probs_rounded(st.layer, st.g, s)
                    if s in (DEN_AT + 1, DEN_AT + 2) and st.prev is not None:
                        reciprocal_diag(st.g - 1, s - DEN_AT - 1)
                    if s == 0 and st.layer == 1 and st.prev is None:
                        shift_to_row(1, st.g, st.parity)
                    if st.phi_g:
                        n = (st.b + 1) * BLOCKS + st.i
                        if s == PHI_AT + 1:
                            act.wait_ge(l_k, (st.b + 1) * BLOCKS + 1)
                            take_phi(n, st.i, free_bank)
                        if s == G_AT + 1:
                            act.wait_ge(l_v, (st.b + 1) * BLOCKS + 1)
                            take_g(n, st.i, free_bank)
                    if st.kv:
                        n, c = st.nth - 1, st.i - 1
                        if s == K_AT:
                            act.wait_ge(s_done, st.g + 2)
                            act.wait_ge(l_phi, (st.b + 1) * BLOCKS + 1)
                            act.wait_ge(l_g, (st.b + 1) * BLOCKS + 1)
                            make_k(n, c, mid_new[:, 1 - st.parity])
                        if s == V_AT + 1:
                            take_v(n, c, free_bank)
                if st.ends:
                    take_output(st.g, st.parity)
                if st.turn:
                    take_q_whole(st.g + 2, 1, scores[:, 1, 0:QB])
                    take_q_hi(1, st.parity, scores[:, 1, 0:QB])
                if st.ends:
                    reciprocal_diag(st.g, 0)
                    reciprocal_diag(st.g, 1)

            def turn(b):
                _, g, nth, parity = end_of_layer0(b)
                act.wait_ge(s_done, g + 3)
                make_k(nth, BLOCKS - 1, mid_new[:, parity])
                take_v(nth, BLOCKS - 1, scores[:, 1, QB:GC])

            run_all(act, turn, block_program)

        @block.vector
        def _(dve):
            def reduce_piece(n, piece, src):
                t, c = piece
                dve.wait_ge(s_rough, n + 1)
                nc.vector.reduce_max(piece_max[:, t, c:c + 1], src, AX.X).then_inc(s_reduced, 1)

            def shift(g, parity):
                dve.wait_ge(s_reduced, (g + 1) * PIECES + 1)
                nc.vector.reduce_max(query_max[:], piece_max[:], AX.X).then_inc(s_qmax, 1)
                dve.wait_ge(s_qmax, g + 1)
                nc.vector.tensor_tensor(
                    diag[:, parity].rearrange("p (t c) -> p t c", c=P),
                    neg_ident[:].unsqueeze(1).to_broadcast([P, SUB, P]),
                    query_max[:].unsqueeze(2).to_broadcast([P, SUB, P]), ALU.mult).then_inc(s_diag, 1)

            def split(g, s):
                n = g * GROUPS + s
                dve.wait_ge(s_probs, 2 * n + 6)
                dve.wait_ge(s_used, n + 1)
                nc.vector.tensor_tensor(probs_lo[:, s % LO_BUFS], probs[:, s % 2], rd(probs_hi[:, s % HI_BUFS]),
                                        ALU.subtract).then_inc(s_split, 1)

            def shift_scores(g, nth, parity, s):
                dve.wait_ge(s_scores, g * GROUPS + s + 1)
                dve.wait_ge(s_plus, added(g, s - 2) if s >= 2 else g * ADDS + s + 1)
                dve.wait_ge(s_split, g * GROUPS + s + 1)
                dve.wait_ge(s_row_sb, g + 1)
                nc.vector.tensor_tensor(
                    probs[:, s % 2].rearrange("p (h c) -> p h c", c=QB),
                    scores[:, s % 2].rearrange("p (h c) -> p h c", c=QB),
                    shift_rows[:, parity].unsqueeze(1).to_broadcast([P, TPG, QB]), ALU.add).then_inc(s_shifted, 1)

            def reciprocals(g, parity):
                dve.wait_ge(s_den, g + 2)
                den = acc_out[:, parity, 0:2 * SUB].rearrange("p (t c) -> p t c", c=2)[:, :, 0:1]
                nc.vector.reciprocal(rcol[:].unsqueeze(2), den).then_inc(s_rcol, 1)
                dve.wait_ge(s_rcol, g + 1)
                nc.vector.tensor_copy(rparts[:, 0], rcol[:]).then_inc(s_rparts, 1)
                dve.wait_ge(s_rparts, 2 * g + 1)
                nc.vector.tensor_tensor(rparts[:, 1], rcol[:], rd(rparts[:, 0]), ALU.subtract).then_inc(s_rparts, 1)

            def normalise(layer, g, nth, parity):
                dve.wait_ge(s_rden, g + 1)
                if layer == 0:
                    nc.vector.tensor_tensor(o_sb[:], o_sb[:], acc_out[:, parity], ALU.mult).then_inc(s_norm, 1)
                else:
                    dve.wait_ge(s_stored, 16 * nth + 16)
                    nc.vector.tensor_tensor(result[:], o_sb[:], acc_out[:, parity], ALU.mult).then_inc(s_norm, 1)

            def finish(layer, g, nth, parity):
                dve.wait_ge(s_xres, 16 * g + 16)
                if layer == 0:
                    dve.wait_ge(s_wy, nth + 1)
                    dve.wait_ge(s_mid, 16 * nth + 16)
                    src, dst, bias = acc_out[:, parity], mid_new[:, parity], OUT_B
                else:
                    dve.wait_ge(s_norm, g + 1)
                    src, dst, bias = result[:], result[:], V_B
                nc.vector.scalar_tensor_tensor(out=dst, in0=src, scalar=bias, in1=x_res[:],
                                               op0=ALU.add, op1=ALU.add).then_inc(s_done, 1)

            for free, n in ((s_reduced, 1), (s_probs, 4), (s_split, 2), (s_plus, 2), (s_den, 1),
                            (s_used, HI_BUFS), (s_done, 2), (s_stored, 16),
                            (s_mid, 32), (l_phi, 1), (l_g, 1), (l_k, 1), (l_v, 1)):
                dve.sem_inc(free, n)
            nc.vector.memset(ones[:], 1.0).then_inc(s_set, 1)
            nc.vector.memset(g_bias[:], 0.0).then_inc(s_set, 1)
            dve.wait_ge(s_set, 1)
            nc.vector.tensor_copy(ones_r[:], ones[:]).then_inc(s_set, 1)
            dve.wait_ge(s_const, 16 * CONSTS)
            nc.vector.tensor_scalar(neg_ident[:], idt[:], -1.0, None, ALU.mult).then_inc(s_set, 1)
            dve.wait_ge(s_set, 4)
            dve.wait_ge(s_small, 1)
            nc.vector.tensor_copy(K_S, rough[:, 0:1]).then_inc(s_vec, 1)
            nc.vector.tensor_tensor(OUT_B, rough[:, QB:QB + 1], vec[:, 7:8], ALU.add).then_inc(s_vec, 1)
            dve.wait_ge(s_vec, 2)

            for m, piece in enumerate(pieces):
                reduce_piece(m, piece, four_banks[m % SUB])
            shift(0, 0)

            def block_program(st):
                at = TURN_PIECES_AT if st.turn else PIECES_AT[st.layer]
                m = 0
                for s in range(GROUPS):
                    if st.prev is not None:
                        layer, g, nth, parity = before(st)
                        if s == DEN_AT + 1:
                            reciprocals(g, parity)
                        if s == RDEN_AT + 1:
                            normalise(layer, g, nth, parity)
                        if s == FINISH_AT[layer]:
                            finish(layer, g, nth, parity)
                    if s == DIAG_AT and st.nxt is not None and not st.turn:
                        shift(st.g + 1, 1 - st.parity)
                    if st.layer == 1 and s in SHIFTED:
                        shift_scores(st.g, st.nth, st.parity, s)
                    if st.nxt is not None:
                        for _ in range(min(at[s], 2)):
                            reduce_piece(st.pieces + m, pieces[m], two_banks(m))
                            m += 1
                    if s > 0:
                        split(st.g, s - 1)
                    elif st.prev is not None:
                        split(st.g - 1, GROUPS - 1)
                    if st.nxt is not None and at[s] == 3:
                        reduce_piece(st.pieces + m, pieces[m], two_banks(m))
                        m += 1
                if st.ends:
                    add(dve, st.layer, st.g, st.parity, GROUPS - 2)
                    split(st.g, GROUPS - 1)
                    add(dve, st.layer, st.g, st.parity, GROUPS - 1)
                    fold(dve, st.g, st.parity)
                    reciprocals(st.g, st.parity)
                    normalise(st.layer, st.g, st.nth, st.parity)
                    finish(st.layer, st.g, st.nth, st.parity)

            def turn(b):
                _, g, _, parity = end_of_layer0(b)
                for t, piece in enumerate(last_pieces):
                    reduce_piece((g + 2) * PIECES - SUB + t, piece, four_banks[t])
                shift(g + 1, 1 - parity)

            run_all(dve, turn, block_program)

        @block.gpsimd
        def _(pool):
            def lo_part(dst, w, hi, done):
                nc.gpsimd.tensor_tensor(dst, w, rd(hi), ALU.subtract).then_inc(done, 1)

            def split_q(g, parity, first=False):
                pool.wait_ge(h_q, g + 1)
                if not first:
                    pool.wait_ge(s_probs, (g - 1) * (2 * GROUPS) + 4)
                lo_part(qry_b[:, parity], q_whole[:], qry_a[:, parity], l_q)

            def split_phi(n, c):
                pool.wait_ge(h_phi, n + 1)
                at = cols(phi_a, c)[0:IC]
                lo_part(at, whole[0:IC, 0], at, l_phi)

            def split_g(n, c):
                pool.wait_ge(h_g, n + 1)
                w = whole[:, 1, 0:TPC * IC].rearrange("p (t c) -> p t c", c=IC)
                lo_part(g_part(c, True), w, g_part(c, False), l_g)

            def split_k(n, c):
                pool.wait_ge(h_k, n + 1)
                lo_part(cols(k_lo, c), whole[:, 0], cols(k_hi, c), l_k)

            def split_v(n, c):
                pool.wait_ge(h_v, n + 1)
                lo_part(cols(v_vals[:, N:2 * N], c), whole[:, 1], cols(v_vals[:, 0:N], c), l_v)

            nc.gpsimd.memset(phi_b[0:IC, :].bitcast(F32), 1.0 / IC).then_inc(s_ones, 1)
            split_q(0, 0, first=True)
            for c in range(BLOCKS):
                split_phi(c, c)
                split_g(c, c)

            def block_program(st):
                for s in range(GROUPS):
                    if s < GROUPS - 2 or not st.ends:
                        add(pool, st.layer, st.g, st.parity, s)
                    if s == FOLD_AT and st.prev is not None:
                        fold(pool, st.g - 1, 1 - st.parity)
                    if s == Q_LO_AT and st.nxt is not None:
                        split_q(st.g + 1, 1 - st.parity)
                    if s == PHI_AT + 1 and st.phi_g:
                        split_phi((st.b + 1) * BLOCKS + st.i, st.i)
                    if s == G_AT + 1 and st.phi_g:
                        split_g((st.b + 1) * BLOCKS + st.i, st.i)
                    if s == K_LO_AT and st.kv:
                        split_k(st.nth - 1, st.i - 1)
                    if s == V_LO_AT and st.kv:
                        split_v(st.nth - 1, st.i - 1)
            def turn(b):
                _, _, nth, _ = end_of_layer0(b)
                split_k(nth, BLOCKS - 1)
                split_v(nth, BLOCKS - 1)

            run_all(pool, turn, block_program)


def kernel(x, L0_conv_g_w, L0_conv_g_b, L0_conv_theta_w, L0_conv_theta_b, L0_conv_phi_w, L0_conv_phi_b,
           L0_conv_W_w, L0_conv_W_b, L1_conv_Wq, L1_conv_bq, L1_conv_Wk, L1_conv_bk, L1_conv_Wv, L1_conv_bv):
    import numpy as np
    import concourse.bacc as bacc
    from concourse.bass_utils import run_bass_kernel_spmd

    def turned(w):
        return np.ascontiguousarray(np.asarray(w).T)

    def column(v):
        return np.asarray(v).reshape(-1, 1)

    shape = np.shape(x)
    arrays = {
        "x": np.ascontiguousarray(np.asarray(x).reshape(shape[0], shape[1], -1)),
        "wT_theta": turned(L0_conv_theta_w), "b_theta": column(L0_conv_theta_b),
        "wT_phi": turned(L0_conv_phi_w), "b_phi": column(L0_conv_phi_b),
        "wT_g": turned(L0_conv_g_w), "b_g": column(L0_conv_g_b),
        "wT_out": turned(L0_conv_W_w), "b_out": column(L0_conv_W_b),
        "wT_q": turned(L1_conv_Wq), "b_q": column(L1_conv_bq),
        "w_k": np.asarray(L1_conv_Wk), "b_k": column(L1_conv_bk),
        "wT_v": turned(L1_conv_Wv), "b_v": column(L1_conv_bv),
        "ident": np.eye(P, dtype=np.float32),
    }
    nc = bacc.Bacc("TRN2", target_bir_lowering=False, num_devices=1)
    args = {n: nc.dram_tensor(n, a.shape, mybir.dt.from_np(a.dtype), kind="ExternalInput").ap()
            for n, a in arrays.items()}
    out = nc.dram_tensor("out", arrays["x"].shape, F32, kind="ExternalOutput").ap()
    build(nc, out=out, **args)
    r = run_bass_kernel_spmd(nc, [arrays], core_ids=[0])
    return r.results[0]["out"].reshape(shape)
```
